# Optimizing a Trainium2 kernel written in Bass

```python
import numpy as np
import jax
import jax.numpy as jnp

def _softmax(x, axis=-1):
    return jax.nn.softmax(x, axis=axis)

def _gelu(x):
    return jax.nn.gelu(x, approximate=True)

def _silu(x):
    return jax.nn.silu(x)

def _sigmoid(x):
    return jax.nn.sigmoid(x)

def _layernorm(x, axis=-1, eps=1e-05):
    m = jnp.mean(x, axis=axis, keepdims=True)
    v = jnp.var(x, axis=axis, keepdims=True)
    return (x - m) / jnp.sqrt(v + eps)

def _scatter_add(tgt, idx, src, axis=0):
    return tgt.at[idx].add(src)

def _segment_sum(src, seg, n):
    return jax.ops.segment_sum(src, seg, n)
kernel_name = 'mk_conv_preact_d2_conv_nchw192_r2_4ca40f'

def setup_inputs(seed: int=0):
    np.random.seed(seed)
    _w = jnp.asarray

    def _rec_inputs():
        import jax
        import jax.numpy as jnp
        _gk = jax.random.key(seed)
        x = -4.65e-05 + 0.9999 * jax.random.normal(jax.random.fold_in(_gk, 1), (4, 96, 128, 128), jnp.float32)
        return x
    x = _rec_inputs()

    def _L0_conv_setup():
        import jax, jax.numpy as jnp
        import numpy as np
        from jax import lax
        EPS_LN = 1e-05
        EPS_NORM = 1e-12
        NUM_HEADS = 8
        KV_HEADS = 2
        REP = NUM_HEADS // KV_HEADS

        def _layernorm_c(x, w, b):
            mu = x.mean(axis=1, keepdims=True)
            var = ((x - mu) ** 2).mean(axis=1, keepdims=True)
            return (x - mu) / jnp.sqrt(var + EPS_LN) * w[None, :, None, None] + b[None, :, None, None]

        def _conv1x1(x, w):
            return jnp.einsum('bchw,oc->bohw', x, w)

        def _dwconv3x3(x, w):
            C = x.shape[1]
            return lax.conv_general_dilated(x, w, window_strides=(1, 1), padding='SAME', dimension_numbers=('NCHW', 'OIHW', 'NCHW'), feature_group_count=C)

        def _l2norm(x):
            n = jnp.sqrt(jnp.sum(x * x, axis=-1, keepdims=True))
            return x / jnp.maximum(n, EPS_NORM)
        key = jax.random.key(seed)
        ks = jax.random.split(key, 8)
        b, dim, h, w = (4, 96, 128, 128)
        kv_ch = 2 * dim // REP
        return {'x': jax.random.normal(ks[0], (b, dim, h, w), jnp.float32), 'ln_w': jnp.ones((dim,), jnp.float32), 'ln_b': jnp.zeros((dim,), jnp.float32), 'q_w': jax.random.normal(ks[1], (dim, dim), jnp.float32) * 0.02, 'q_dw': jax.random.normal(ks[2], (dim, 1, 3, 3), jnp.float32) * 0.1, 'kv_w': jax.random.normal(ks[3], (kv_ch, dim), jnp.float32) * 0.02, 'kv_dw': jax.random.normal(ks[4], (kv_ch, 1, 3, 3), jnp.float32) * 0.1, 'proj_w': jax.random.normal(ks[5], (dim, dim), jnp.float32) * 0.02, 'temperature': jnp.ones((NUM_HEADS, 1, 1), jnp.float32)}
    _L0_conv_all = _L0_conv_setup()
    _L0_conv_in = {k: v for k, v in _L0_conv_all.items() if k in ('ln_w', 'ln_b', 'q_w', 'q_dw', 'kv_w', 'kv_dw', 'proj_w', 'temperature')}
    del _L0_conv_all

    def _L1_conv_setup():
        import jax, jax.numpy as jnp
        import numpy as np

        def _conv(x, w, padding, dilation=(1, 1)):
            return jax.lax.conv_general_dilated(x, w, window_strides=(1, 1), padding=padding, rhs_dilation=dilation, dimension_numbers=('NCHW', 'OIHW', 'NCHW'))
        key = jax.random.key(seed)
        ks = jax.random.split(key, 6)
        C, B, H, W = (96, 8, 64, 64)
        x = jax.random.normal(ks[0], (B, C, H, W), dtype=jnp.float32)
        w1 = jax.random.normal(ks[1], (C, C, 1, 1), dtype=jnp.float32) / np.sqrt(C)
        w3 = jax.random.normal(ks[2], (C, C, 3, 3), dtype=jnp.float32) / np.sqrt(C * 9)
        w5 = jax.random.normal(ks[3], (C, C, 5, 5), dtype=jnp.float32) / np.sqrt(C * 25)
        wd = jax.random.normal(ks[4], (C, C, 3, 3), dtype=jnp.float32) / np.sqrt(C * 9)
        wf = jax.random.normal(ks[5], (C, 4 * C, 1, 1), dtype=jnp.float32) / np.sqrt(4 * C)
        return {'x': x, 'w1': w1, 'w3': w3, 'w5': w5, 'wd': wd, 'wf': wf}
    _L1_conv_all = _L1_conv_setup()
    _L1_conv_in = {k: v for k, v in _L1_conv_all.items() if k in ('w1', 'w3', 'w5', 'wd', 'wf')}
    del _L1_conv_all
    return {'x': x, 'L0_conv_ln_w': _L0_conv_in['ln_w'], 'L0_conv_ln_b': _L0_conv_in['ln_b'], 'L0_conv_q_w': _L0_conv_in['q_w'], 'L0_conv_q_dw': _L0_conv_in['q_dw'], 'L0_conv_kv_w': _L0_conv_in['kv_w'], 'L0_conv_kv_dw': _L0_conv_in['kv_dw'], 'L0_conv_proj_w': _L0_conv_in['proj_w'], 'L0_conv_temperature': _L0_conv_in['temperature'], 'L1_conv_w1': _L1_conv_in['w1'], 'L1_conv_w3': _L1_conv_in['w3'], 'L1_conv_w5': _L1_conv_in['w5'], 'L1_conv_wd': _L1_conv_in['wd'], 'L1_conv_wf': _L1_conv_in['wf']}

def reference(x, L0_conv_ln_w, L0_conv_ln_b, L0_conv_q_w, L0_conv_q_dw, L0_conv_kv_w, L0_conv_kv_dw, L0_conv_proj_w, L0_conv_temperature, L1_conv_w1, L1_conv_w3, L1_conv_w5, L1_conv_wd, L1_conv_wf):
    import jax
    import jax.numpy as jnp

    def _L0_conv_ref(x, ln_w, ln_b, q_w, q_dw, kv_w, kv_dw, proj_w, temperature):
        import jax, jax.numpy as jnp
        import numpy as np
        from jax import lax
        EPS_LN = 1e-05
        EPS_NORM = 1e-12
        NUM_HEADS = 8
        KV_HEADS = 2
        REP = NUM_HEADS // KV_HEADS

        def _layernorm_c(x, w, b):
            mu = x.mean(axis=1, keepdims=True)
            var = ((x - mu) ** 2).mean(axis=1, keepdims=True)
            return (x - mu) / jnp.sqrt(var + EPS_LN) * w[None, :, None, None] + b[None, :, None, None]

        def _conv1x1(x, w):
            return jnp.einsum('bchw,oc->bohw', x, w)

        def _dwconv3x3(x, w):
            C = x.shape[1]
            return lax.conv_general_dilated(x, w, window_strides=(1, 1), padding='SAME', dimension_numbers=('NCHW', 'OIHW', 'NCHW'), feature_group_count=C)

        def _l2norm(x):
            n = jnp.sqrt(jnp.sum(x * x, axis=-1, keepdims=True))
            return x / jnp.maximum(n, EPS_NORM)
        b, c, h, w = x.shape
        xn = _layernorm_c(x, ln_w, ln_b)
        q = _dwconv3x3(_conv1x1(xn, q_w), q_dw)
        kv = _dwconv3x3(_conv1x1(xn, kv_w), kv_dw)
        k, v = jnp.split(kv, 2, axis=1)
        hw = h * w
        ch = c // NUM_HEADS
        q = q.reshape(b, NUM_HEADS, ch, hw)
        k = k.reshape(b, KV_HEADS, ch, hw)
        v = v.reshape(b, KV_HEADS, ch, hw)
        k = jnp.repeat(k, REP, axis=1)
        v = jnp.repeat(v, REP, axis=1)
        q = _l2norm(q)
        k = _l2norm(k)
        attn = jnp.einsum('bhcn,bhdn->bhcd', q, k) * temperature[None]
        attn = jax.nn.softmax(attn, axis=-1)
        out = jnp.einsum('bhcd,bhdn->bhcn', attn, v)
        out = out.reshape(b, c, h, w)
        return _conv1x1(out, proj_w)

    def _L1_conv_ref(x, w1, w3, w5, wd, wf):
        import jax, jax.numpy as jnp
        import numpy as np

        def _conv(x, w, padding, dilation=(1, 1)):
            return jax.lax.conv_general_dilated(x, w, window_strides=(1, 1), padding=padding, rhs_dilation=dilation, dimension_numbers=('NCHW', 'OIHW', 'NCHW'))
        x1 = _conv(x, w1, padding=[(0, 0), (0, 0)])
        x2 = _conv(x, w3, padding=[(1, 1), (1, 1)])
        x3 = _conv(x, w5, padding=[(2, 2), (2, 2)])
        x4 = _conv(x, wd, padding=[(2, 2), (2, 2)], dilation=(2, 2))
        out = jnp.concatenate([x1, x2, x3, x4], axis=1)
        return _conv(out, wf, padding=[(0, 0), (0, 0)])

    def _gn(v, G=32, eps=1e-05):
        B_, C_, H_, W_ = v.shape
        g = v.reshape(B_, G, C_ // G, H_, W_)
        m = jnp.mean(g, axis=(2, 3, 4), keepdims=True)
        s = jnp.var(g, axis=(2, 3, 4), keepdims=True)
        return ((g - m) / jnp.sqrt(s + eps)).reshape(v.shape)

    def _ln_c(v, eps=1e-06):
        m = jnp.mean(v, axis=1, keepdims=True)
        s = jnp.var(v, axis=1, keepdims=True)
        return (v - m) / jnp.sqrt(s + eps)

    def _ln_t(v, eps=1e-05):
        m = jnp.mean(v, axis=-1, keepdims=True)
        s = jnp.var(v, axis=-1, keepdims=True)
        return (v - m) / jnp.sqrt(s + eps)

    def _to_tokens(v):
        B_, C_, H_, W_ = v.shape
        return v.reshape(B_, C_, H_ * W_).transpose(0, 2, 1)

    def _from_tokens(t, like):
        B_, C_, H_, W_ = like.shape
        return t.transpose(0, 2, 1).reshape(B_, C_, H_, W_)
    x = x + _L0_conv_ref(_gn(x), L0_conv_ln_w, L0_conv_ln_b, L0_conv_q_w, L0_conv_q_dw, L0_conv_kv_w, L0_conv_kv_dw, L0_conv_proj_w, L0_conv_temperature)
    x = x + _L1_conv_ref(_gn(x), L1_conv_w1, L1_conv_w3, L1_conv_w5, L1_conv_wd, L1_conv_wf)
    return x

_drawn_inputs = setup_inputs


def setup_inputs(seed=0):
    import zlib

    import numpy as np

    out = dict(_drawn_inputs(seed))
    spreads = {'L0_conv_ln_w': (1.0, 0.6), 'L0_conv_ln_b': (0.0, 0.8), 'L0_conv_temperature': (1.0, 0.6)}
    factors = {'L0_conv_q_w': 8.0,
     'L0_conv_q_dw': 8.0,
     'L0_conv_kv_w': 8.0,
     'L0_conv_kv_dw': 8.0,
     'L0_conv_proj_w': 8.0}
    for name, (base, spread) in spreads.items():
        noise = np.random.default_rng([zlib.crc32(name.encode()), seed]).standard_normal(out[name].shape)
        drawn = base * np.exp(spread * noise) if base else spread * noise
        out[name] = jnp.asarray(drawn.astype(out[name].dtype))
    for name, factor in factors.items():
        out[name] = (out[name] * factor).astype(out[name].dtype)
    return out
```

```python
from contextlib import ExitStack

import concourse.bass as bass
from concourse import mybir


def build_program(nc, x, ln_w, ln_b, q_w, q_dw, kv_w, kv_dw, proj_w, temperature, w1, w3, w5, wd, wf, out):
    f32, f16, i32 = mybir.dt.float32, mybir.dt.float16, mybir.dt.int32
    ALU = mybir.AluOpType
    ACT = mybir.ActivationFunctionType
    AX = mybir.AxisListType

    B, C, H, W = x.shape
    P = 128
    HEADS, GROUPS = 8, 32
    CG = C // GROUPS
    KV = kv_w.shape[0]
    KC = KV // 2
    HD = C // HEADS
    CO = C + KV
    QK = C + KC
    PX = H * W
    EPS = 1e-5
    BANK = 512

    AR = BANK // W
    AT = H // AR
    NP = CO + C
    DC = 6
    DK = CO // DC
    DM = 3 * DC
    BW = 129
    GR = 8
    GS = H // GR
    VP = 32
    SR = 8
    SS = H // SR
    SI = SR + 4
    WP = W + 4
    TAPS = 25
    XP = 2
    YSCALE = 64.0
    WTOP = 4096.0

    ctx = ExitStack()
    with ctx:
        def sb(name, shape, dt=f32):
            return ctx.enter_context(nc.sbuf_tensor(name, shape, dt))

        def sem(name):
            return ctx.enter_context(nc.semaphore(name))

        X = sb("X", [C, (H + 2 * XP) * W])
        Q = sb("Q", [P, CO, H])
        work = sb("work", [P, 9600])
        wh = sb("wh", [C, TAPS, C], f16)
        wl = sb("wl", [C, TAPS, C], f16)
        y1 = sb("y1", [C, 2, BANK])
        proj = sb("proj", [C, NP])
        V = sb("V", [P, 3, 3 * CO])
        band = sb("band", [P, BW])
        ident = sb("ident", [P, P])
        center = sb("center", [C, C])
        gmean = sb("gmean", [C, C])
        pT = sb("pT", [C, C])
        cbias = sb("cbias", [P, CO])
        mblk = sb("mblk", [P, 4, C])
        stats = sb("stats", [C, AT, 6])
        small = sb("small", [P, 64])
        edge = sb("edge", [C, 4, SS])
        emask = sb("emask", [C, 2, SS])
        vr = sb("vr", [P, 2, AR])
        sd = sb("sd", [P, 2, AR])
        rr = sb("rr", [P, 2, AR])
        epsc = sb("epsc", [P, 1])
        att = sb("att", [P, 4 * P])
        amask = sb("amask", [C, KC])
        ps = ctx.enter_context(nc.psum_tensor("ps", [P, 8, BANK], f32))

        sq = work[:, 0:2 * AR * C].rearrange("p (i r c) -> p i r c", i=2, r=AR)
        pq = work[:, 768:768 + 2 * AR * CO].rearrange("p (i r c) -> p i r c", i=2, r=AR)
        T = work[:, 2000:2000 + 2 * DM * BW].rearrange("p (i m x) -> p i m x", i=2, m=DM)
        vT = work[:, 2000:2000 + AT * P]
        S = work[:, 7000:7000 + 2 * GR * QK].rearrange("p (i r c) -> p i r c", i=2, r=GR)
        vs = work[:, 8980:8980 + 2 * GR * VP].rearrange("p (i r c) -> p i r c", i=2, r=GR)
        y2 = work[0:C, 0:SI * W]
        hl0 = SI * W
        hlw = SI * WP // 2
        hl = [[work[0:C, hl0 + (2 * i + j) * hlw:hl0 + (2 * i + j + 1) * hlw].bitcast(f16)
               .rearrange("p (r w) -> p r w", w=WP) for j in range(2)] for i in range(2)]
        ob0 = hl0 + 4 * hlw
        ob = [work[0:C, ob0 + i * SR * W:ob0 + (i + 1) * SR * W] for i in range(2)]
        assert ob0 + 2 * SR * W <= 9600
        Qf = Q[:, :, :].rearrange("p c h -> p (c h)")
        raw5 = Qf[0:C, 0:2400]
        raw3 = Qf[0:C, 2400:2400 + 864]
        rawd = Qf[0:C, 3264:3264 + 864]
        raw1 = Qf[0:C, 4128:4128 + 96]
        rawf = Qf[0:C, 4224:4224 + 384]
        wfT = Qf[0:C, 4608:4608 + 384].rearrange("p (b c) -> p b c", b=4)
        folded = Qf[0:C, 4992:4992 + 2400]
        rawdw = Qf[:, 7392:7392 + 9 * CO].rearrange("p (m d) -> p m d", d=3)
        qw = Qf[0:C, 8700:8700 + 96]
        kvw = Qf[0:KV, 8796:8796 + 96]
        pw = Qf[0:C, 8892:8892 + 96]
        wT = Qf[0:C, 9000:9000 + CO]
        wTs = Qf[0:C, 9150:9150 + CO]
        lnbb = Qf[0:C, 9300:9300 + P]
        res = Qf[:, 9500:9500 + 3 * 43].rearrange("p (k i) -> p k i", k=3)
        onesr = Qf[0:1, 9700:9700 + P]

        def col(i, n=C):
            return small[0:n, i:i + 1]
        LNW, LNB, TEMP, MEAN, VAR, MG, DEV, VG, RSTD, SA, SBI, AMAX, POW, WSC, OSC, DIAG, RN, NMX, DEN, RDEN, RES0 = range(21)
        RT, GMAX = 24, 25

        def pair(name):
            return [sem(name + "0"), sem(name + "1")]

        s_w = sem("weights_loaded")
        s_x = sem("image_loaded")
        s_pool0 = sem("constants_made")
        s_pt = sem("setup_products")
        s_dv = sem("setup_vector_steps")
        s_st = sem("image_vector_steps")
        s_pst = sem("image_products")
        s_exp = sem("softmax_exponentials")
        s_y1 = pair("normed_tile")
        s_pa = pair("projected_tile")
        s_sq = pair("squared_tile")
        s_vr = pair("variance_sum")
        s_sd = pair("deviation_of_tile")
        s_rr = pair("rstd_of_tile")
        s_sqrt = sem("square_roots")
        s_pq = pair("scaled_tile")
        s_q = pair("stored_tile")
        s_T = pair("band_matrices")
        s_dw = pair("depthwise_chunk")
        s_qd = pair("stored_chunk")
        s_S = pair("gram_strip")
        s_vs = pair("value_strip")
        s_g = pair("gram_products")
        s_vt = pair("value_transposed")
        s_vc = pair("value_copied")
        s_o = pair("attention_tile")
        s_x1 = pair("x1_tile")
        s_bn = sem("x1_statistics")
        s_y2 = sem("normed_rows")
        s_h = sem("high_part")
        s_l = sem("low_part")
        s_cv = pair("convolved_tile")
        s_ob = pair("output_tile")
        s_out = pair("output_written")

        NLOADS = 13
        NPOOL = 23
        N_MEAN, N_VG, N_AFF = 1, 4, 7
        N_DIAG, N_SCALED, N_NMX, N_ATT, N_MBLK = (N_AFF + k for k in (4, 6, 9, 11, 15))
        NST, NPST = N_MBLK + N_AFF + 4, 6
        block = ctx.enter_context(nc.Block())

        class Steps:
            def __init__(self, s, base=0):
                self.s, self.base, self.n = s, base, 0

            def done(self, ins):
                ins.then_inc(self.s, 1)
                self.n += 1

            def value(self):
                return self.base + self.n

        @block.sync
        def _(sync):
            loads = [
                (qw, q_w), (kvw, kv_w), (pw, proj_w),
                (raw1, w1.rearrange("m c a b -> m (c a b)")),
                (raw3, w3.rearrange("m c a b -> m (c a b)")),
                (raw5, w5.rearrange("m c a b -> m (c a b)")),
                (rawd, wd.rearrange("m c a b -> m (c a b)")),
                (rawf, wf.rearrange("m c a b -> m (c a b)")),
                (col(LNW), ln_w.rearrange("(c o) -> c o", o=1)),
                (col(LNB), ln_b.rearrange("(c o) -> c o", o=1)),
                (col(TEMP), bass.AP(tensor=temperature.tensor, offset=0, ap=[[1, HEADS], [0, HD], [1, 1]])),
                (rawdw[:, 0:3 * C, :].rearrange("p m d -> p (m d)"),
                 bass.AP(tensor=q_dw.tensor, offset=0, ap=[[0, P], [1, 9 * C]])),
                (rawdw[:, 3 * C:3 * CO, :].rearrange("p m d -> p (m d)"),
                 bass.AP(tensor=kv_dw.tensor, offset=0, ap=[[0, P], [1, 9 * KV]])),
            ]
            for dst, src in loads:
                sync.dma_start(dst, src).then_inc(s_w, 16)
            assert len(loads) == NLOADS
            sync.dma_start(X[:, XP * W:(XP + H) * W], x[0].rearrange("c h w -> c (h w)")).then_inc(s_x, 16)

            def store_strips(b):
                with sync.Fori(0, SS // 2) as s2:
                    for i in range(2):
                        sync.wait_ge(s_ob[i], (b * (SS // 2) + s2) * 2 + 2)
                        sync.dma_start(out[bass.ds(b, 1), :, bass.ds((s2 * 2 + i) * SR, SR), :]
                                       .rearrange("o c h w -> (o c) (h w)"), ob[i]).then_inc(s_out[i], 16)

            with sync.Fori(0, B - 1) as b:
                store_strips(b)
                sync.wait_ge(s_y2, (b + 1) * SS * 3)
                sync.dma_start(X[:, XP * W:(XP + H) * W],
                               x[bass.ds(b + 1, 1)].rearrange("o c h w -> (o c) (h w)")).then_inc(s_x, 16)
            store_strips(B - 1)
            for i in range(2):
                sync.wait_ge(s_out[i], B * (SS // 2) * 16)

        @block.gpsimd
        def _(pool):
            n = [0]

            def link(ins):
                n[0] += 1
                ins.then_inc(s_pool0, 1)
                pool.wait_ge(s_pool0, n[0])
            link(pool.memset(ident[:], 0.0))
            link(pool.affine_select(out=ident[:], in_=ident[:], compare_op=ALU.not_equal, fill=1.0, base=0,
                                    pattern=[[-1, P]], channel_multiplier=1))
            link(pool.memset(center[:], -1.0 / C))
            link(pool.affine_select(out=center[:], in_=center[:], compare_op=ALU.not_equal, fill=1.0 - 1.0 / C, base=0,
                                    pattern=[[-1, C]], channel_multiplier=1))
            g3 = gmean[:].rearrange("p (g k) -> p g k", k=CG)
            link(pool.memset(gmean[:], 1.0 / CG))
            link(pool.affine_select(out=g3, in_=g3, compare_op=ALU.is_ge, fill=0.0, base=0,
                                    pattern=[[-CG, GROUPS], [0, CG]], channel_multiplier=1))
            link(pool.affine_select(out=g3, in_=g3, compare_op=ALU.is_ge, fill=0.0, base=CG - 1,
                                    pattern=[[CG, GROUPS], [0, CG]], channel_multiplier=-1))
            link(pool.memset(band[:], 1.0))
            link(pool.affine_select(out=band[:], in_=band[:], compare_op=ALU.is_ge, fill=0.0, base=1,
                                    pattern=[[-1, BW]], channel_multiplier=1))
            link(pool.affine_select(out=band[:], in_=band[:], compare_op=ALU.is_ge, fill=0.0, base=1,
                                    pattern=[[1, BW]], channel_multiplier=-1))
            link(pool.memset(res, 0.0))
            link(pool.affine_select(out=res, in_=res, compare_op=ALU.not_equal, fill=1.0, base=0,
                                    pattern=[[-1, 3], [-3, 43]], channel_multiplier=1))
            m3 = amask[:].rearrange("p (g k) -> p g k", g=2)
            link(pool.memset(amask[:], 0.0))
            link(pool.affine_select(out=m3[:, 0, :], in_=m3[:, 0, :], compare_op=ALU.is_ge, fill=-1e30, base=C // 2 - 1,
                                    pattern=[[0, KC // 2]], channel_multiplier=-1))
            link(pool.affine_select(out=m3[:, 1, :], in_=m3[:, 1, :], compare_op=ALU.is_ge, fill=-1e30, base=-(C // 2),
                                    pattern=[[0, KC // 2]], channel_multiplier=1))
            link(pool.memset(emask[:], 1.0))
            link(pool.memset(emask[:, 0, 0:1], 0.0))
            link(pool.memset(emask[:, 1, SS - 1:SS], 0.0))
            link(pool.memset(onesr, 1.0))
            link(pool.memset(X[:, 0:XP * W], 0.0))
            link(pool.memset(X[:, (XP + H) * W:], 0.0))
            link(pool.memset(vs, 0.0))
            link(pool.memset(epsc[:], EPS))
            assert n[0] == NPOOL

            with pool.Fori(0, B) as b:
                with pool.Fori(0, AT // 2) as t2:
                    for i in range(2):
                        pool.wait_ge(s_pq[i], b * (AT // 2) + t2 + 1)
                        pool.tensor_tensor(Q[:, :, bass.ds((t2 * 2 + i) * AR, AR)].rearrange("p c r -> p r c"), pq[:, i],
                                           cbias[:].unsqueeze(1).broadcast_to([P, AR, CO]), ALU.add).then_inc(s_q[i], 1)
                with pool.Fori(0, DK // 2) as k2:
                    for i in range(2):
                        pool.wait_ge(s_dw[i], b * (DK // 2) + k2)
                        for j in range(2):
                            pool.wait_ge(s_out[j], b * (SS // 2) * 16)
                        taps = V[:, :, bass.ds((k2 * 2 + i) * DM, DM)].rearrange("p j m -> p m j").unsqueeze(2)
                        mask = band[:].rearrange("p (i j) -> p i j", j=3).unsqueeze(1)
                        pool.tensor_tensor(T[:, i].rearrange("p m (i j) -> p m i j", j=3),
                                           taps.broadcast_to([P, DM, BW // 3, 3]), mask.broadcast_to([P, DM, BW // 3, 3]),
                                           ALU.mult).then_inc(s_T[i], 1)

        @block.tensor
        def _(pe):
            setup = Steps(s_pt)
            mm, tr = nc.tensor.matmul, nc.tensor.transpose
            idc = ident[0:C, 0:C]
            pe.wait_ge(s_w, NLOADS * 16)
            pe.wait_ge(s_pool0, NPOOL)
            setup.done(tr(ps[0:C, 0, 0:C], qw, idc))
            setup.done(tr(ps[0:C, 0, C:CO], kvw, ident[0:KV, 0:KV]))
            setup.done(tr(ps[0:C, 0, CO:NP], pw, idc))
            for k in range(4):
                setup.done(tr(ps[0:C, 1, k * C:(k + 1) * C], rawf[:, k * C:(k + 1) * C], idc))
            pe.wait_ge(s_dv, 5)
            setup.done(mm(ps[0:C, 2, 0:CO], center[:], wTs, start=True, stop=True))
            setup.done(mm(ps[:, 3, 0:CO], lnbb, wT, start=True, stop=True))
            k3, k5, kd = (a.rearrange("m (c t) -> m c t", c=C) for a in (raw3, raw5, rawd))
            for t in range(TAPS):
                dy, dx = divmod(t, 5)
                terms = [(k5[:, :, t], 2)]
                if 1 <= dy <= 3 and 1 <= dx <= 3:
                    terms.append((k3[:, :, (dy - 1) * 3 + dx - 1], 1))
                if dy % 2 == 0 and dx % 2 == 0:
                    terms.append((kd[:, :, dy // 2 * 3 + dx // 2], 3))
                if t == TAPS // 2:
                    terms.append((raw1, 0))
                for m, (w, br) in enumerate(terms):
                    last = mm(ps[0:C, (4 + t // 5) % 8, t % 5 * C:(t % 5 + 1) * C], w, wfT[:, br, :],
                              start=m == 0, stop=m == len(terms) - 1)
                if t % 5 == 4:
                    setup.done(last)
            pe.wait_ge(s_dv, 14)
            setup.done(tr(ps[0:1, 1, 0:C], col(AMAX), idc))
            pe.wait_ge(s_dv, 16)
            setup.done(mm(ps[0:C, 2, 0:1], onesr[0:1, 0:C], small[0:1, GMAX:GMAX + 1], start=True, stop=True))

            def group_means(st, first):
                pe.wait_ge(s_st, first + N_MEAN)
                st.done(mm(ps[0:C, 7, 0:1], gmean[:], col(MEAN), start=True, stop=True))
                pe.wait_ge(s_st, first + N_VG)
                st.done(mm(ps[0:C, 7, 0:1], gmean[:], col(VG), start=True, stop=True))

            with pe.Fori(0, B) as b:
                st = Steps(s_pst, b * NPST)
                group_means(st, b * NST)
                with pe.Fori(0, AT // 2) as t2:
                    for i in range(2):
                        n = b * (AT // 2) + t2
                        pe.wait_ge(s_y1[i], n + 1)
                        pe.wait_ge(s_sq[i], n)
                        pe.wait_ge(s_pq[i], n)
                        for r in range(AR):
                            last = mm(ps[:, 2 * i + r // 2, r % 2 * 256:r % 2 * 256 + NP], y1[:, i, r * W:(r + 1) * W],
                                      proj[:], start=True, stop=True)
                        last.then_inc(s_pa[i], 1)
                with pe.Fori(0, DK // 2) as k2:
                    for i in range(2):
                        n = b * (DK // 2) + k2
                        for j in range(2):
                            pe.wait_ge(s_q[j], (b + 1) * (AT // 2))
                        pe.wait_ge(s_T[i], n + 1)
                        pe.wait_ge(s_qd[i], n)
                        for c in range(DC):
                            o = ps[:, 4 + 2 * i + c // 3, c % 3 * H:(c % 3 + 1) * H]
                            src = Q[:, bass.ds((k2 * 2 + i) * DC + c, 1), :].rearrange("p o h -> p (o h)")
                            mm(o, T[:, i, 3 * c + 1, 0:W], src, start=True, stop=False)
                            mm(o[:, 1:H], T[:, i, 3 * c, 0:W], src[:, 0:H - 1], start=False, stop=False)
                            last = mm(o[:, 0:H - 1], T[:, i, 3 * c + 2, 0:W], src[:, 1:H], start=False, stop=True)
                        last.then_inc(s_dw[i], 1)

                def gram(g2, first):
                    for i in range(2):
                        n = b * (GS // 2) + g2
                        pe.wait_ge(s_S[i], n + 1)
                        for r in range(GR):
                            last = mm(ps[0:QK, 0, 0:QK], S[:, i, r, :], S[:, i, r, :],
                                      start=first and i == 0 and r == 0, stop=True, skip_group_check=True)
                        last.then_inc(s_g[i], 1)
                        pe.wait_ge(s_vs[i], n + 1)
                        pe.wait_ge(s_vc[i], n)
                        for j in range(GR // 4):
                            last = tr(ps[:, 1 + i, j * P:(j + 1) * P],
                                      vs[:, i, 4 * j:4 * j + 4, :].rearrange("p r c -> p (r c)"), ident[:])
                        last.then_inc(s_vt[i], 1)
                gram(0, True)
                with pe.Fori(1, GS // 2) as g2:
                    gram(g2, False)
                pe.wait_ge(s_st, b * NST + N_SCALED)
                st.done(tr(ps[0:QK, 3, 0:QK], att[0:QK, P:P + QK], ident[0:QK, 0:QK]))
                pe.wait_ge(s_st, b * NST + N_ATT)
                st.done(mm(ps[:, 3, 0:C], att[0:C, 3 * P:4 * P], pT[:], start=True, stop=True))
                with pe.Fori(0, AT // 2) as t2:
                    for i in range(2):
                        for j in range(2):
                            pe.wait_ge(s_vc[j], (b + 1) * (GS // 2))
                        pe.wait_ge(s_st, b * NST + N_MBLK)
                        pe.wait_ge(s_x1[i], b * (AT // 2) + t2)
                        for j in range(AR):
                            last = mm(ps[0:C, 5 + i, j * W:(j + 1) * W], mblk[:, j, :],
                                      vT[:, bass.ds((t2 * 2 + i) * P, P)], start=True, stop=True)
                        last.then_inc(s_o[i], 1)
                group_means(st, b * NST + N_MBLK)
                assert st.n == NPST
                with pe.Fori(0, SS // 2) as s2:
                    for i in range(2):
                        n = b * (SS // 2) + s2
                        pe.wait_ge(s_l, b * SS + s2 * 2 + i + 1)
                        pe.wait_ge(s_ob[i], 2 * n)
                        for j in range(2):
                            m = 0
                            for t in range(TAPS):
                                dy, dx = divmod(t, 5)
                                for part, wt in ((0, wh), (0, wl), (1, wh)):
                                    last = mm(ps[0:C, 2 * i + j, :], wt[:, t, :],
                                              hl[i][part][:, 4 * j + dy:4 * j + dy + 4, dx:dx + W],
                                              start=m == 0, stop=m == 3 * TAPS - 1)
                                    m += 1
                            last.then_inc(s_cv[i], 1)

        @block.scalar
        def _(act):
            act.wait_ge(s_pool0, NPOOL)

            def deviation(products):
                act.wait_ge(s_pst, products)
                act.activation(col(RSTD), ps[0:C, 7, 0:1], ACT.Sqrt, bias=epsc[0:C]).then_inc(s_sqrt, 1)

            with act.Fori(0, B) as b:
                act.wait_ge(s_x, (b + 1) * 16)
                deviation(b * NPST + 2)
                act.wait_ge(s_st, b * NST + N_AFF)
                with act.Fori(0, AT // 2) as t2:
                    n = b * (AT // 2) + t2
                    for i in range(2):
                        act.wait_ge(s_pa[i], n)
                        act.activation(y1[:, i, :], X[:, bass.ds((t2 * 2 + i) * BANK + XP * W, BANK)], ACT.Identity,
                                       bias=col(SBI), scale=col(SA)).then_inc(s_y1[i], 1)
                    for i in range(2):
                        act.wait_ge(s_pa[i], n + 1)
                        act.wait_ge(s_vr[i], n)
                        act.activation(sq[:, i], ps[:, 2 * i:2 * i + 2, :].rearrange("p b (r c) -> p (b r) c", r=2)[:, :, CO:NP],
                                       ACT.Square, scale=float(C) ** -0.5).then_inc(s_sq[i], 1)
                    for i in range(2):
                        act.wait_ge(s_vr[i], n + 1)
                        act.wait_ge(s_rr[i], n)
                        act.activation(sd[:, i, :], vr[:, i, :], ACT.Sqrt, bias=epsc[:]).then_inc(s_sd[i], 1)
                with act.Fori(0, DK // 2) as k2:
                    for i in range(2):
                        act.wait_ge(s_dw[i], b * (DK // 2) + k2 + 1)
                        act.activation(Q[:, bass.ds((k2 * 2 + i) * DC, DC), :].rearrange("p (k c) h -> p k (c h)", k=2),
                                       ps[:, 4 + 2 * i:6 + 2 * i, 0:3 * H], ACT.Copy).then_inc(s_qd[i], 1)
                for i in range(2):
                    act.wait_ge(s_qd[i], (b + 1) * (DK // 2))
                with act.Fori(0, GS // 2) as g2:
                    n = b * (GS // 2) + g2
                    for i in range(2):
                        act.wait_ge(s_vt[i], n)
                        act.activation(vs[:, i, :, 0:KC], Q[:, QK:CO, bass.ds((g2 * 2 + i) * GR, GR)].rearrange("p c r -> p r c"),
                                       ACT.Copy).then_inc(s_vs[i], 1)
                    for i in range(2):
                        act.wait_ge(s_vt[i], n + 1)
                        act.activation(vT[:, bass.ds((g2 * 2 + i) * 2 * P, 2 * P)], ps[:, 1 + i, 0:2 * P], ACT.Copy).then_inc(s_vc[i], 1)
                act.wait_ge(s_st, b * NST + N_DIAG)
                act.activation(col(DIAG, QK), col(DIAG, QK), ACT.Sqrt).then_inc(s_sqrt, 1)
                act.wait_ge(s_st, b * NST + N_NMX)
                act.activation(att[0:C, 2 * P + 32:2 * P + 32 + KC], att[0:C, 2 * P:2 * P + KC], ACT.Exp, bias=col(NMX),
                               accum_out=col(DEN)).then_inc(s_exp, 1)
                deviation(b * NPST + 6)
                act.wait_ge(s_st, (b + 1) * NST)
                with act.Fori(0, SS // 2) as s2:
                    for i in range(2):
                        m = s2 * 2 + i
                        n = b * SS + m
                        act.wait_ge(s_l, n)
                        for lo, hi, bias, scale in ((0, 2, edge[:, 1, bass.ds(m, 1)], edge[:, 0, bass.ds(m, 1)]),
                                                    (2, SI - 2, col(SBI), col(SA)),
                                                    (SI - 2, SI, edge[:, 3, bass.ds(m, 1)], edge[:, 2, bass.ds(m, 1)])):
                            act.activation(y2[:, lo * W:hi * W], X[:, bass.ds(m * SR * W + lo * W, (hi - lo) * W)],
                                           ACT.Identity, bias=bias, scale=scale).then_inc(s_y2, 1)
                        act.wait_ge(s_y2, n * 3 + 3)
                        act.wait_ge(s_cv[i], (b * (SS // 2) + s2) * 2)
                        act.activation(hl[i][0][:, :, 2:2 + W], y2.rearrange("p (r w) -> p r w", w=W), ACT.Copy).then_inc(s_h, 1)

        @block.vector
        def _(dve):
            v = nc.vector
            setup = Steps(s_dv)

            def link(steps, ins):
                steps.done(ins)
                dve.wait_ge(steps.s, steps.value())
            dve.wait_ge(s_w, NLOADS * 16)
            dve.wait_ge(s_pool0, NPOOL)
            dve.wait_ge(s_pt, 7)
            link(setup, v.tensor_copy(wT, ps[0:C, 0, 0:CO]))
            link(setup, v.tensor_copy(pT[:], ps[0:C, 0, CO:NP]))
            link(setup, v.tensor_copy(wfT.rearrange("p b c -> p (b c)"), ps[0:C, 1, 0:4 * C]))
            link(setup, v.tensor_scalar(wTs, wT, col(LNW), None, ALU.mult))
            link(setup, v.tensor_scalar(lnbb, ident[0:C, :], 0.0, col(LNB), ALU.mult, ALU.add))
            dve.wait_ge(s_pt, 9)
            link(setup, v.tensor_copy(proj[:, 0:CO], ps[0:C, 2, 0:CO]))
            link(setup, v.tensor_copy(proj[:, CO:NP], center[:]))
            link(setup, v.tensor_copy(cbias[:], ps[:, 3, 0:CO]))
            for k in range(5):
                dve.wait_ge(s_pt, 10 + k)
                link(setup, v.tensor_copy(folded[:, k * 5 * C:(k + 1) * 5 * C], ps[0:C, (4 + k) % 8, 0:5 * C]))
            link(setup, v.tensor_reduce(col(AMAX), folded, AX.X, ALU.max, apply_absolute_value=True))
            dve.wait_ge(s_pt, 15)
            link(setup, v.tensor_reduce(small[0:1, GMAX:GMAX + 1], ps[0:1, 1, 0:C], AX.X, ALU.max))
            link(setup, v.tensor_scalar(small[0:1, GMAX:GMAX + 1], small[0:1, GMAX:GMAX + 1], 1e-30, None, ALU.max))
            dve.wait_ge(s_pt, 16)
            link(setup, v.tensor_copy(col(AMAX), ps[0:C, 2, 0:1]))
            link(setup, v.tensor_scalar(col(POW).bitcast(i32), col(AMAX).bitcast(i32), 0x7F800000, None, ALU.bitwise_and))
            link(setup, v.reciprocal(col(WSC), col(POW)))
            link(setup, v.tensor_scalar(col(WSC), col(WSC), WTOP, None, ALU.mult))
            link(setup, v.tensor_scalar(col(OSC), col(POW), 1.0 / (WTOP * YSCALE), None, ALU.mult))
            whf, wlf = (a[:].rearrange("p t c -> p (t c)") for a in (wh, wl))
            link(setup, v.tensor_scalar(whf, folded, col(WSC), None, ALU.mult))
            link(setup, v.scalar_tensor_tensor(wlf, folded, col(WSC), whf, ALU.mult, ALU.subtract))
            for k in range(3):
                link(setup, v.tensor_reduce(small[:, RES0 + k:RES0 + k + 1], res[:, k, :], AX.X, ALU.add))
            for j in range(3):
                for d in range(3):
                    r = RES0 + (d + j - 1) % 3
                    if d == 0:
                        link(setup, v.tensor_scalar(V[:, j, :], rawdw[:, :, d], small[:, r:r + 1], None, ALU.mult))
                    else:
                        link(setup, v.scalar_tensor_tensor(V[:, j, :], rawdw[:, :, d], small[:, r:r + 1], V[:, j, :],
                                                           ALU.mult, ALU.add))
            link(setup, v.memset(mblk[:], 0.0))
            link(setup, v.memset(att[:], 0.0))

            def affine(st, pst, root, tiles, scale):
                dve.wait_ge(s_bn, tiles)
                v.memset(col(MG), 0.0)
                link(st, v.bn_aggr(small[0:C, MEAN:MEAN + 2], stats[:].rearrange("p t s -> p (t s)")))
                dve.wait_ge(s_pst, pst + 1)
                link(st, v.tensor_copy(col(MG), ps[0:C, 7, 0:1]))
                link(st, v.tensor_tensor(col(DEV), col(MEAN), col(MG), ALU.subtract))
                link(st, v.scalar_tensor_tensor(col(VG), col(DEV), col(DEV), col(VAR), ALU.mult, ALU.add))
                dve.wait_ge(s_sqrt, root)
                link(st, v.reciprocal(col(RSTD), col(RSTD)))
                link(st, v.tensor_scalar(col(SA), col(RSTD), scale, None, ALU.mult))
                st.done(v.scalar_tensor_tensor(col(SBI), col(MG), -1.0, col(SA), ALU.mult, ALU.mult))

            with dve.Fori(0, B) as b:
                st = Steps(s_st, b * NST)
                with dve.Fori(0, AT) as t:
                    dve.wait_ge(s_x, (b + 1) * 16)
                    v.bn_stats(stats[:, bass.ds(t, 1), :].rearrange("p o s -> p (o s)"),
                               X[:, bass.ds(t * BANK + XP * W, BANK)]).then_inc(s_bn, 1)
                affine(st, b * NPST, b * 3 + 1, b * 2 * AT + AT, 1.0)
                with dve.Fori(0, AT // 2) as t2:
                    n = b * (AT // 2) + t2
                    for i in range(2):
                        dve.wait_ge(s_sq[i], n + 1)
                        v.tensor_reduce(vr[:, i, :], sq[:, i], AX.X, ALU.add).then_inc(s_vr[i], 1)
                    for i in range(2):
                        dve.wait_ge(s_sd[i], n + 1)
                        v.reciprocal(rr[:, i, :], sd[:, i, :]).then_inc(s_rr[i], 1)
                    for i in range(2):
                        dve.wait_ge(s_rr[i], n + 1)
                        dve.wait_ge(s_q[i], n)
                        v.tensor_tensor(pq[:, i], ps[:, 2 * i:2 * i + 2, :].rearrange("p b (r c) -> p (b r) c", r=2)[:, :, 0:CO],
                                        rr[:, i, :].unsqueeze(2).broadcast_to([P, AR, CO]), ALU.mult).then_inc(s_pq[i], 1)
                with dve.Fori(0, GS // 2) as g2:
                    for i in range(2):
                        for j in range(2):
                            dve.wait_ge(s_qd[j], (b + 1) * (DK // 2))
                        dve.wait_ge(s_g[i], b * (GS // 2) + g2)
                        v.tensor_copy(S[:, i], Q[:, 0:QK, bass.ds((g2 * 2 + i) * GR, GR)].rearrange("p c r -> p r c")).then_inc(s_S[i], 1)
                for i in range(2):
                    dve.wait_ge(s_g[i], (b + 1) * (GS // 2))
                link(st, v.tensor_copy(att[0:QK, 0:QK], ps[0:QK, 0, 0:QK]))
                link(st, v.tensor_tensor(att[0:QK, P:P + QK], att[0:QK, 0:QK], ident[0:QK, 0:QK], ALU.mult))
                link(st, v.tensor_reduce(col(DIAG, QK), att[0:QK, P:P + QK], AX.X, ALU.add))
                link(st, v.tensor_scalar(col(DIAG, QK), col(DIAG, QK), 1e-24, None, ALU.max))
                dve.wait_ge(s_sqrt, b * 3 + 2)
                link(st, v.reciprocal(col(RN, QK), col(DIAG, QK)))
                link(st, v.tensor_scalar(att[0:QK, P:P + QK], att[0:QK, 0:QK], col(RN, QK), None, ALU.mult))
                dve.wait_ge(s_pst, b * NPST + 3)
                logits = att[0:C, 2 * P:2 * P + KC]
                link(st, v.tensor_scalar(logits, ps[0:C, 3, C:QK], col(RN), col(TEMP), ALU.mult, ALU.mult))
                link(st, v.tensor_tensor(logits, logits, amask[:], ALU.add))
                link(st, v.tensor_reduce(col(NMX), logits, AX.X, ALU.max, negate=True))
                dve.wait_ge(s_exp, b + 1)
                link(st, v.reciprocal(col(RDEN), col(DEN)))
                link(st, v.tensor_scalar(att[0:C, 3 * P:4 * P].rearrange("p (j c) -> p j c", j=4)[:, :, 0:KC],
                                         att[0:C, 2 * P + 32:2 * P + 32 + KC].unsqueeze(1).broadcast_to([C, 4, KC]),
                                         col(RDEN), None, ALU.mult))
                dve.wait_ge(s_pst, b * NPST + 4)
                for j in range(AR):
                    st.done(v.tensor_copy(mblk[VP * j:VP * (j + 1), j, :], ps[VP * j:VP * (j + 1), 3, 0:C]))
                with dve.Fori(0, AT // 2) as t2:
                    n = b * (AT // 2) + t2
                    for i in range(2):
                        xt = X[:, bass.ds((t2 * 2 + i) * BANK + XP * W, BANK)]
                        dve.wait_ge(s_o[i], n + 1)
                        v.tensor_tensor(xt, ps[0:C, 5 + i, :], xt, ALU.add).then_inc(s_x1[i], 1)
                    for i in range(2):
                        xt = X[:, bass.ds((t2 * 2 + i) * BANK + XP * W, BANK)]
                        dve.wait_ge(s_x1[i], n + 1)
                        v.bn_stats(stats[:, bass.ds(t2 * 2 + i, 1), :].rearrange("p o s -> p (o s)"), xt).then_inc(s_bn, 1)
                affine(st, b * NPST + 4, b * 3 + 3, (b + 1) * 2 * AT, YSCALE)
                dve.wait_ge(s_st, st.value())
                for k in range(4):
                    st.done(v.tensor_scalar(edge[:, k, :], emask[:, k // 2, :], col(SA if k % 2 == 0 else SBI), None, ALU.mult))
                assert st.n == NST, st.n

                def low(s2, i):
                    m = b * SS + s2 * 2 + i
                    dve.wait_ge(s_h, m + 1)
                    v.tensor_tensor(hl[i][1][:, :, 2:2 + W], y2.rearrange("p (r w) -> p r w", w=W), hl[i][0][:, :, 2:2 + W],
                                    ALU.subtract).then_inc(s_l, 1)

                def evacuate(s2, i):
                    n = b * (SS // 2) + s2
                    dve.wait_ge(s_out[i], n * 16)
                    for j in range(2):
                        dve.wait_ge(s_cv[i], 2 * n + j + 1)
                        v.scalar_tensor_tensor(ob[i][:, j * BANK:(j + 1) * BANK], ps[0:C, 2 * i + j, :], col(OSC),
                                               X[:, bass.ds((s2 * 2 + i) * SR * W + (XP + 4 * j) * W, BANK)],
                                               ALU.mult, ALU.add).then_inc(s_ob[i], 1)
                for i in range(2):
                    for part in range(2):
                        v.memset(hl[i][part][:, :, 0:2], 0.0)
                        v.memset(hl[i][part][:, :, 2 + W:WP], 0.0)
                low(0, 0)
                low(0, 1)
                with dve.Fori(0, SS // 2 - 1) as s2:
                    for i in range(2):
                        evacuate(s2, i)
                        low(s2 + 1, i)
                for i in range(2):
                    evacuate(SS // 2 - 1, i)


_INS = ['x', 'L0_conv_ln_w', 'L0_conv_ln_b', 'L0_conv_q_w', 'L0_conv_q_dw', 'L0_conv_kv_w', 'L0_conv_kv_dw',
        'L0_conv_proj_w', 'L0_conv_temperature', 'L1_conv_w1', 'L1_conv_w3', 'L1_conv_w5', 'L1_conv_wd', 'L1_conv_wf']


def kernel(**inputs):
    import numpy as _np
    import concourse.bacc as _bacc
    from concourse import mybir as _mybir
    from concourse.bass_utils import run_bass_kernel_spmd as _run

    nc = _bacc.Bacc("TRN2", target_bir_lowering=False, num_devices=1)
    arrays, args = {}, []
    for name in _INS:
        a = _np.ascontiguousarray(inputs[name])
        arrays[f"in_{name}_dram"] = a
        args.append(nc.dram_tensor(f"in_{name}_dram", a.shape, _mybir.dt.from_np(a.dtype), kind="ExternalInput").ap())
    shape = inputs['x'].shape
    args.append(nc.dram_tensor("out_0_dram", shape, _mybir.dt.float32, kind="ExternalOutput").ap())
    build_program(nc, *args)
    r = _run(nc, [arrays], core_ids=[0])
    return r.results[0]["out_0_dram"]
```

```python
from contextlib import ExitStack

import concourse.bass as bass
from concourse import mybir


def build_program(nc, x, ln_w, ln_b, q_w, q_dw, kv_w, kv_dw, proj_w, temperature, w1, w3, w5, wd, wf, out):
    f32, f16, i32 = mybir.dt.float32, mybir.dt.float16, mybir.dt.int32
    ALU = mybir.AluOpType
    ACT = mybir.ActivationFunctionType
    AX = mybir.AxisListType

    B, C, H, W = x.shape
    P = 128
    HEADS, GROUPS = 8, 32
    CG = C // GROUPS
    KV = kv_w.shape[0]
    KC = KV // 2
    HD = C // HEADS
    CO = C + KV
    QK = C + KC
    PX = H * W
    EPS = 1e-5
    BANK = 512

    AR = BANK // W
    AT = H // AR
    AD = 4
    NP = CO + C
    DC = 6
    DK = CO // DC
    DM = 3 * DC
    BW = 129
    GR = 8
    GS = H // GR
    VP = 32
    SR = 8
    SS = H // SR
    SI = SR + 4
    WP = W + 4
    TAPS = 25
    XP = 2
    XL = SR * W // BANK
    YSCALE = 64.0
    WTOP = 4096.0

    KIND_TAPS = (2, 3, 3)
    KIND_AT = (0, 2, 5)
    TERMS = (((1, None), (3, None)), ((0, None), (2, 1), (4, 3)), ((0, 1), (2, 3), (4, None)))
    FOLD = [t for kind in TERMS for t in kind]
    HR = SR // 2
    HC = W // 2
    ROWS = [HR + t - 1 for t in KIND_TAPS]
    COLS = [HC + t - 1 for t in KIND_TAPS]
    OUTS = HR * HC
    MEM = [(0, 0), (1, 0), (2, 0), (1, 1), (2, 1), (1, 2), (2, 2), (0, 1), (0, 2)]
    TIME = [(0, 0), (0, 1), (0, 2), (1, 0), (2, 0), (1, 1), (1, 2), (2, 1), (2, 2)]
    PSBANK = dict(zip(TIME, (0, 1, 2, 3, 4, 5, 6, 7, 2)))
    AT_EL, PART_END = {}, 0
    for part in MEM:
        AT_EL[part] = PART_END
        PART_END += ROWS[part[0]] * COLS[part[1]]
    WIDE = AT_EL[(1, 1)]
    HALF = (PART_END + 1) // 2
    TWO_ROWS = [(0, True), (2, True), (4, False), (5, True), (7, False)]
    LOWS = {}
    for rk, ck in MEM:
        if ck == 0:
            LOWS[rk, ck] = [(rt, 0, P, k) for k, (rt, _) in enumerate(TWO_ROWS)
                            if KIND_AT[rk] <= rt < KIND_AT[rk] + KIND_TAPS[rk]]
        else:
            LOWS[rk, ck] = [(rt, KIND_AT[ck], 96, len(TWO_ROWS) + 8 * (ck - 1) + rt)
                            for rt in range(KIND_AT[rk], KIND_AT[rk] + KIND_TAPS[rk])]
    NLOW = len(TWO_ROWS) + 16

    ctx = ExitStack()
    with ctx:
        def sb(name, shape, dt=f32):
            return ctx.enter_context(nc.sbuf_tensor(name, shape, dt))

        START = 4
        counted = []

        def sem(name):
            counted.append(ctx.enter_context(nc.semaphore(name)))
            return counted[-1]

        def plain_sem(name):
            return ctx.enter_context(nc.semaphore(name))

        X = sb("X", [C, (H + 2 * XP) * W])
        Q = sb("Q", [P, CO, H])
        work = sb("work", [P, 6592])
        wh = sb("wh", [P, 8, 8, C], f16)
        wl = sb("wl", [P, 8, 8, C], f16)
        wp = sb("wp", [P, NLOW, C], f16)
        proj = sb("proj", [C, NP])
        V = sb("V", [P, 3, 3 * CO])
        band = sb("band", [P, BW])
        ident = sb("ident", [P, P])
        center = sb("center", [C, C])
        gmean = sb("gmean", [C, C])
        pT = sb("pT", [C, C])
        cbias = sb("cbias", [P, CO])
        stats = sb("stats", [C, AT, 6])
        small = sb("small", [P, 64])
        edge = sb("edge", [C, 4, SS])
        emask = sb("emask", [C, 2, SS])
        vr = sb("vr", [P, AD, AR])
        sd = sb("sd", [P, AD, AR])
        rr = sb("rr", [P, AD, AR])
        epsc = sb("epsc", [P, 1])
        amask = sb("amask", [C, KC])
        ps = ctx.enter_context(nc.psum_tensor("ps", [P, 8, BANK], f32))

        sq = work[:, 0:2 * AR * C].rearrange("p (i r c) -> p i r c", i=2, r=AR)
        pq = work[:, 768:768 + 2 * AR * CO].rearrange("p (i r c) -> p i r c", i=2, r=AR)
        y1 = work[0:C, 4000:4000 + AD * BANK].rearrange("p (i n) -> p i n", i=AD)
        att = work[:, 0:4 * P]
        mblk = work[:, 4 * P:4 * P + 4 * C].rearrange("p (j c) -> p j c", j=4)
        T = work[:, 1940:1940 + 2 * DM * BW].rearrange("p (i m x) -> p i m x", i=2, m=DM)
        vT = work[:, 1940:1940 + AT * P]
        S = work[:, 0:2 * GR * QK].rearrange("p (i r c) -> p i r c", i=2, r=GR)
        vs = work[:, 6040:6040 + 2 * GR * VP].rearrange("p (i r c) -> p i r c", i=2, r=GR)
        Qf = Q[:, :, :].rearrange("p c h -> p (c h)")
        halfs = lambda k: Qf[:, k * HALF:(k + 1) * HALF].bitcast(f16)
        hi = [halfs(i) for i in range(2)]
        hi2 = [halfs(2 + i) for i in range(2)]
        lo = [halfs(4 + i) for i in range(2)]
        low = halfs(6)[0:C]
        y2 = Qf[0:C, 7 * HALF:7 * HALF + SI * WP].rearrange("p (r w) -> p r w", w=WP)
        rsum = Qf[0:C, 7 * HALF + SI * WP:7 * HALF + (SI + ROWS[0]) * WP].rearrange("p (r w) -> p r w", w=WP)
        assert 7 * HALF + (SI + ROWS[0]) * WP <= CO * H
        csum = work[0:C, 0:SI * COLS[0]].rearrange("p (r w) -> p r w", w=COLS[0])
        rcsum = work[0:C, SI * COLS[0]:(SI + ROWS[0]) * COLS[0]].rearrange("p (r w) -> p r w", w=COLS[0])
        ob = work[0:C, 1920:1920 + SR * W]
        mid = [work[0:C, 4000 + i * OUTS:4000 + (i + 1) * OUTS] for i in range(3)]
        part_view = lambda t, part: t[:, AT_EL[part]:AT_EL[part] + ROWS[part[0]] * COLS[part[1]]] \
            .rearrange("p (r w) -> p r w", w=COLS[part[1]])

        def both(t, ck):
            a = AT_EL[1, ck]
            return t[:, a:a + 2 * ROWS[1] * COLS[ck]].rearrange("p (s r w) -> p s r w", s=2, w=COLS[ck])

        def plain_views(t):
            grid = y2.rearrange("p (k s) (j c) -> p c s k j", s=2, c=2)
            return [(both(t[0:C], 1 + c), grid[:, c]) for c in range(2)]

        def sum_views(t):
            grid = rsum.rearrange("p k (j c) -> p c k j", c=2)
            return [(part_view(t[0:C], (0, 1 + c)), grid[:, c]) for c in range(2)] + \
                   [(both(t[0:C], 0), csum.rearrange("p (k s) j -> p s k j", s=2)), (part_view(t[0:C], (0, 0)), rcsum)]
        raw5 = Qf[0:C, 0:2400]
        raw3 = Qf[0:C, 2400:2400 + 864]
        rawd = Qf[0:C, 3264:3264 + 864]
        raw1 = Qf[0:C, 4128:4128 + 96]
        rawf = Qf[0:C, 4224:4224 + 384]
        wfT = Qf[0:C, 4608:4608 + 384].rearrange("p (b c) -> p b c", b=4)
        folded = Qf[0:C, 4992:4992 + 2400]
        rawdw = Qf[:, 7392:7392 + 9 * CO].rearrange("p (m d) -> p m d", d=3)
        rfold = Qf[0:C, 9900:9900 + 8 * 5 * C].rearrange("p (r x c) -> p r x c", r=8, x=5)
        fast = Qf[0:C, 0:64 * C].rearrange("p (r x c) -> p r x c", r=8, x=8)
        qw = Qf[0:C, 8700:8700 + 96]
        kvw = Qf[0:KV, 8796:8796 + 96]
        pw = Qf[0:C, 8892:8892 + 96]
        wT = Qf[0:C, 9000:9000 + CO]
        wTs = Qf[0:C, 9150:9150 + CO]
        lnbb = Qf[0:C, 9300:9300 + P]
        res = Qf[:, 9500:9500 + 3 * 43].rearrange("p (k i) -> p k i", k=3)
        onesr = Qf[0:1, 9700:9700 + P]

        def col(i, n=C):
            return small[0:n, i:i + 1]
        LNW, LNB, TEMP, MEAN, VAR, MG, DEV, VG, RSTD, SA, SBI, AMAX, POW, WSC, OSC, DIAG, RN, NMX, DEN, RDEN, RES0 = range(21)
        RT, GMAX = 24, 25

        def pair(name):
            return [sem(name + "0"), sem(name + "1")]

        s_w = plain_sem("weights_loaded")
        s_x = pair("rows_loaded")
        s_pool0 = plain_sem("constants_made")
        s_pt = plain_sem("setup_products")
        s_dv = plain_sem("setup_vector_steps")
        s_st = sem("image_vector_steps")
        s_pst = sem("image_products")
        s_exp = sem("softmax_exponentials")
        s_y1 = sem("normed_tile")
        s_pa = sem("projected_tile")
        s_sq = sem("squared_tile")
        s_vr = sem("variance_sum")
        s_sd = sem("deviation_of_tile")
        s_rr = sem("rstd_of_tile")
        s_sqrt = sem("square_roots")
        s_pq = sem("scaled_tile")
        s_q = sem("stored_tile")
        s_T = sem("band_matrices")
        s_dw = sem("depthwise_chunk")
        s_qd = sem("stored_chunk")
        s_S = pair("gram_strip")
        s_vs = pair("value_strip")
        s_g = pair("gram_products")
        s_vt = pair("value_transposed")
        s_vc = pair("value_copied")
        s_o = pair("attention_tile")
        s_x1 = pair("x1_tile")
        s_bn = sem("x1_statistics")
        s_y2 = sem("normed_rows")
        s_rs = sem("row_sums")
        s_sum = sem("all_sums")
        s_h = sem("high_parts")
        s_l = sem("low_parts")
        s_ext = pair("parts_placed")
        EXT = 8 * 16
        NPLACES = 24
        s_cv = sem("convolved_part")
        s_m0 = sem("shared_part_copied")
        s_mid = sem("partial_outputs")
        s_res = sem("residual_added")
        s_out = sem("output_written")
        SV = 10
        s_wt = plain_sem("weights_placed")

        NLOADS = 13
        N_AMAX, N_SPLIT = 30, 40
        NPOOL = 22
        N_MEAN, N_VG, N_AFF = 1, 4, 7
        N_DIAG, N_SCALED, N_NMX, N_ATT, N_MBLK = (N_AFF + k for k in (4, 6, 9, 11, 15))
        NST, NPST = N_MBLK + N_AFF + 4, 6
        block = ctx.enter_context(nc.Block())

        class Steps:
            def __init__(self, s, base=0):
                self.s, self.base, self.n = s, base, 0

            def done(self, ins):
                ins.then_inc(self.s, 1)
                self.n += 1

            def value(self):
                return self.base + self.n

        @block.sync
        def _(sync):
            loads = [
                (qw, q_w), (kvw, kv_w), (pw, proj_w),
                (raw1, w1.rearrange("m c a b -> m (c a b)")),
                (raw3, w3.rearrange("m c a b -> m (c a b)")),
                (raw5, w5.rearrange("m c a b -> m (c a b)")),
                (rawd, wd.rearrange("m c a b -> m (c a b)")),
                (rawf, wf.rearrange("m c a b -> m (c a b)")),
                (col(LNW), ln_w.rearrange("(c o) -> c o", o=1)),
                (col(LNB), ln_b.rearrange("(c o) -> c o", o=1)),
                (col(TEMP), bass.AP(tensor=temperature.tensor, offset=0, ap=[[1, HEADS], [0, HD], [1, 1]])),
                (rawdw[:, 0:3 * C, :].rearrange("p m d -> p (m d)"),
                 bass.AP(tensor=q_dw.tensor, offset=0, ap=[[0, P], [1, 9 * C]])),
                (rawdw[:, 3 * C:3 * CO, :].rearrange("p m d -> p (m d)"),
                 bass.AP(tensor=kv_dw.tensor, offset=0, ap=[[0, P], [1, 9 * KV]])),
            ]
            for s_ in counted:
                sync.sem_inc(s_, START)
            for dst, src in loads:
                sync.dma_start(dst, src).then_inc(s_w, 16)
            assert len(loads) == NLOADS
            def load_rows(image, m):
                sync.dma_start(X[:, bass.ds(m * SR * W + XP * W, SR * W)] if not isinstance(m, int) else
                               X[:, (m * SR + XP) * W:((m + 1) * SR + XP) * W],
                               x[image, :, m * SR:(m + 1) * SR, :].rearrange("o c h w -> (o c) (h w)")).then_inc(s_x[m % 2], 16)
            for m in range(SS):
                load_rows(slice(0, 1), m)
            sync.wait_ge(s_dv, N_SPLIT)
            places = [(wh[C:P], wh[0:32]), (wl[C:P], wh[32:64])]
            for k, (rt, second) in enumerate(TWO_ROWS):
                for row in range(1 + second):
                    for ct in range(2):
                        q = 2 * row + ct
                        places.append((wp[32 * q:32 * q + 32, k, :], wh[64:C, rt + row, ct, :]))
            for ck in (1, 2):
                for q in range(3):
                    at = len(TWO_ROWS) + 8 * (ck - 1)
                    places.append((wp[32 * q:32 * q + 32, at:at + 8, :], wh[64:C, :, KIND_AT[ck] + q, :]))
            for dst, src in places:
                sync.dma_start(dst, src).then_inc(s_wt, 16)
            assert len(places) == NPLACES

            def place_low(b, m, i):
                sync.wait_ge(s_h, (b * SS + m) * 6 + 6 + START)
                sync.dma_start(hi2[i][0:C, 0:PART_END], hi[i][0:C, 0:PART_END]).then_inc(s_ext[i], 16)
                sync.wait_ge(s_l, (b * SS + m) * 6 + 6 + START)
                copies = [(hi[i][C:P], 0, 0, 0, PART_END), (hi2[i][C:P], 32, 0, 0, PART_END),
                          (lo[i][0:32], 64, 0, 0, PART_END), (lo[i][32:64], 64, 1, 0, PART_END - 1),
                          (lo[i][64:96], 64, COLS[0], 0, WIDE), (lo[i][96:P], 64, COLS[0] + 1, 0, WIDE),
                          (lo[i][64:96], 64, 2, WIDE, PART_END - 2)]
                for dst, channel, shift, start, end in copies:
                    sync.dma_start(dst[:, start:end], low[channel:channel + 32, start + shift:end + shift]).then_inc(s_ext[i], 16)

            with sync.Fori(0, B) as b:
                place_low(b, 0, 0)
                place_low(b, 1, 1)
                for m in range(SS):
                    i = m % 2
                    with sync.If(b < B - 1):
                        sync.wait_ge(s_res, b * SS + m + 1 + START)
                        sync.wait_ge(s_y2, (b * SS + min(m + 1, SS - 1) + 1) * 3 + START)
                        load_rows(bass.ds((b + 1) % B, 1), m)
                    sync.wait_ge(s_mid, (b * SS + m + 1) * SV + START)
                    sync.dma_start(out[bass.ds(b, 1), :, m * SR:(m + 1) * SR, :].rearrange("o c h w -> (o c) (h w)"),
                                   ob).then_inc(s_out, 16)
                    if m < SS - 2:
                        place_low(b, m + 2, i)
            sync.wait_ge(s_out, B * SS * 16 + START)

        @block.gpsimd
        def _(pool):
            n = [0]

            def link(ins):
                n[0] += 1
                ins.then_inc(s_pool0, 1)
                pool.wait_ge(s_pool0, n[0])
            link(pool.memset(ident[:], 0.0))
            link(pool.affine_select(out=ident[:], in_=ident[:], compare_op=ALU.not_equal, fill=1.0, base=0,
                                    pattern=[[-1, P]], channel_multiplier=1))
            link(pool.memset(center[:], -1.0 / C))
            link(pool.affine_select(out=center[:], in_=center[:], compare_op=ALU.not_equal, fill=1.0 - 1.0 / C, base=0,
                                    pattern=[[-1, C]], channel_multiplier=1))
            g3 = gmean[:].rearrange("p (g k) -> p g k", k=CG)
            link(pool.memset(gmean[:], 1.0 / CG))
            link(pool.affine_select(out=g3, in_=g3, compare_op=ALU.is_ge, fill=0.0, base=0,
                                    pattern=[[-CG, GROUPS], [0, CG]], channel_multiplier=1))
            link(pool.affine_select(out=g3, in_=g3, compare_op=ALU.is_ge, fill=0.0, base=CG - 1,
                                    pattern=[[CG, GROUPS], [0, CG]], channel_multiplier=-1))
            link(pool.memset(band[:], 1.0))
            link(pool.affine_select(out=band[:], in_=band[:], compare_op=ALU.is_ge, fill=0.0, base=1,
                                    pattern=[[-1, BW]], channel_multiplier=1))
            link(pool.affine_select(out=band[:], in_=band[:], compare_op=ALU.is_ge, fill=0.0, base=1,
                                    pattern=[[1, BW]], channel_multiplier=-1))
            link(pool.memset(res, 0.0))
            link(pool.affine_select(out=res, in_=res, compare_op=ALU.not_equal, fill=1.0, base=0,
                                    pattern=[[-1, 3], [-3, 43]], channel_multiplier=1))
            m3 = amask[:].rearrange("p (g k) -> p g k", g=2)
            link(pool.memset(amask[:], 0.0))
            link(pool.affine_select(out=m3[:, 0, :], in_=m3[:, 0, :], compare_op=ALU.is_ge, fill=-1e30, base=C // 2 - 1,
                                    pattern=[[0, KC // 2]], channel_multiplier=-1))
            link(pool.affine_select(out=m3[:, 1, :], in_=m3[:, 1, :], compare_op=ALU.is_ge, fill=-1e30, base=-(C // 2),
                                    pattern=[[0, KC // 2]], channel_multiplier=1))
            link(pool.memset(emask[:], 1.0))
            link(pool.memset(emask[:, 0, 0:1], 0.0))
            link(pool.memset(emask[:, 1, SS - 1:SS], 0.0))
            link(pool.memset(onesr, 1.0))
            link(pool.memset(X[:, 0:XP * W], 0.0))
            link(pool.memset(X[:, (XP + H) * W:], 0.0))
            link(pool.memset(epsc[:], EPS))
            assert n[0] == NPOOL

            with pool.Fori(0, B) as b:
                with pool.Fori(0, AT // 2) as t2:
                    for i in range(2):
                        pool.wait_ge(s_pq, b * AT + t2 * 2 + i + 1 + START)
                        pool.tensor_tensor(Q[:, :, bass.ds((t2 * 2 + i) * AR, AR)].rearrange("p c r -> p r c"), pq[:, i],
                                           cbias[:].unsqueeze(1).broadcast_to([P, AR, CO]), ALU.add).then_inc(s_q, 1)
                with pool.Fori(0, SS) as m:
                    pool.wait_ge(s_mid, (b * SS + m) * SV + 6 + START)
                    pool.tensor_tensor(ob, ob, X[:, bass.ds(m * SR * W + XP * W, SR * W)], ALU.add).then_inc(s_res, 1)

        @block.tensor
        def _(pe):
            setup = Steps(s_pt)
            mm, tr = nc.tensor.matmul, nc.tensor.transpose
            idc = ident[0:C, 0:C]
            pe.wait_ge(s_w, NLOADS * 16)
            pe.wait_ge(s_pool0, NPOOL)
            setup.done(tr(ps[0:C, 0, 0:C], qw, idc))
            setup.done(tr(ps[0:C, 0, C:CO], kvw, ident[0:KV, 0:KV]))
            setup.done(tr(ps[0:C, 0, CO:NP], pw, idc))
            for k in range(4):
                setup.done(tr(ps[0:C, 1, k * C:(k + 1) * C], rawf[:, k * C:(k + 1) * C], idc))
            pe.wait_ge(s_dv, 5)
            setup.done(mm(ps[0:C, 2, 0:CO], center[:], wTs, start=True, stop=True))
            setup.done(mm(ps[:, 3, 0:CO], lnbb, wT, start=True, stop=True))
            k3, k5, kd = (a.rearrange("m (c t) -> m c t", c=C) for a in (raw3, raw5, rawd))
            for t in range(TAPS):
                dy, dx = divmod(t, 5)
                terms = [(k5[:, :, t], 2)]
                if 1 <= dy <= 3 and 1 <= dx <= 3:
                    terms.append((k3[:, :, (dy - 1) * 3 + dx - 1], 1))
                if dy % 2 == 0 and dx % 2 == 0:
                    terms.append((kd[:, :, dy // 2 * 3 + dx // 2], 3))
                if t == TAPS // 2:
                    terms.append((raw1, 0))
                for m, (w, br) in enumerate(terms):
                    last = mm(ps[0:C, (4 + t // 5) % 8, t % 5 * C:(t % 5 + 1) * C], w, wfT[:, br, :],
                              start=m == 0, stop=m == len(terms) - 1)
                if t % 5 == 4:
                    setup.done(last)
            pe.wait_ge(s_dv, N_AMAX)
            setup.done(tr(ps[0:1, 1, 0:C], col(AMAX), idc))
            pe.wait_ge(s_dv, N_AMAX + 2)
            setup.done(mm(ps[0:C, 2, 0:1], onesr[0:1, 0:C], small[0:1, GMAX:GMAX + 1], start=True, stop=True))

            pe.wait_ge(s_wt, NPLACES * 16)

            def group_means(st, first):
                pe.wait_ge(s_st, first + N_MEAN + START)
                st.done(mm(ps[0:C, 7, 0:1], gmean[:], col(MEAN), start=True, stop=True))
                pe.wait_ge(s_st, first + N_VG + START)
                st.done(mm(ps[0:C, 7, 0:1], gmean[:], col(VG), start=True, stop=True))

            with pe.Fori(0, B) as b:
                st = Steps(s_pst, b * NPST)
                group_means(st, b * NST)
                with pe.Fori(0, AT // AD) as t4:
                    for i in range(AD):
                        n = b * AT + t4 * AD + i
                        pe.wait_ge(s_y1, n + 1 + START)
                        pe.wait_ge(s_pq, n + 1 - AD + START)
                        for r in range(AR):
                            last = mm(ps[:, 2 * i + r // 2, r % 2 * 256:r % 2 * 256 + NP], y1[:, i, r * W:(r + 1) * W],
                                      proj[:], start=True, stop=True)
                        last.then_inc(s_pa, 1)
                with pe.Fori(0, DK // 2) as k2:
                    for i in range(2):
                        n = b * DK + k2 * 2 + i
                        pe.wait_ge(s_q, (b + 1) * AT + START)
                        pe.wait_ge(s_T, n + 1 + START)
                        pe.wait_ge(s_qd, n - 1 + START)
                        for c in range(DC):
                            o = ps[:, 4 + 2 * i + c // 3, c % 3 * H:(c % 3 + 1) * H]
                            src = Q[:, bass.ds((k2 * 2 + i) * DC + c, 1), :].rearrange("p o h -> p (o h)")
                            mm(o, T[:, i, 3 * c + 1, 0:W], src, start=True, stop=False)
                            mm(o[:, 1:H], T[:, i, 3 * c, 0:W], src[:, 0:H - 1], start=False, stop=False)
                            last = mm(o[:, 0:H - 1], T[:, i, 3 * c + 2, 0:W], src[:, 1:H], start=False, stop=True)
                        last.then_inc(s_dw, 1)

                def gram(g2, first):
                    for i in range(2):
                        n = b * (GS // 2) + g2
                        pe.wait_ge(s_S[i], n + 1 + START)
                        for r in range(GR):
                            last = mm(ps[0:QK, 0, 0:QK], S[:, i, r, :], S[:, i, r, :],
                                      start=first and i == 0 and r == 0, stop=True, skip_group_check=True)
                        last.then_inc(s_g[i], 1)
                        pe.wait_ge(s_vs[i], n + 1 + START)
                        pe.wait_ge(s_vc[i], n + START)
                        for j in range(GR // 4):
                            last = tr(ps[:, 1 + i, j * P:(j + 1) * P],
                                      vs[:, i, 4 * j:4 * j + 4, :].rearrange("p r c -> p (r c)"), ident[:])
                        last.then_inc(s_vt[i], 1)
                gram(0, True)
                with pe.Fori(1, GS // 2) as g2:
                    gram(g2, False)
                pe.wait_ge(s_st, b * NST + N_SCALED + START)
                st.done(tr(ps[0:QK, 3, 0:QK], att[0:QK, P:P + QK], ident[0:QK, 0:QK]))
                pe.wait_ge(s_st, b * NST + N_ATT + START)
                st.done(mm(ps[:, 3, 0:C], att[0:C, 3 * P:4 * P], pT[:], start=True, stop=True))
                with pe.Fori(0, AT // 2) as t2:
                    for i in range(2):
                        for j in range(2):
                            pe.wait_ge(s_vc[j], (b + 1) * (GS // 2) + START)
                        pe.wait_ge(s_st, b * NST + N_MBLK + START)
                        pe.wait_ge(s_x1[i], b * (AT // 2) + t2 + START)
                        for j in range(AR):
                            last = mm(ps[0:C, 5 + i, j * W:(j + 1) * W], mblk[:, j, :],
                                      vT[:, bass.ds((t2 * 2 + i) * P, P)], start=True, stop=True)
                        last.then_inc(s_o[i], 1)
                group_means(st, b * NST + N_MBLK)
                assert st.n == NPST
                with pe.Fori(0, SS // 2) as m2:
                    for i in range(2):
                        m = b * SS + m2 * 2 + i
                        for q, part in enumerate(TIME):
                            rk, ck = part
                            h, h2, l = (part_view(t[i], part) for t in (hi, hi2, lo))
                            window = lambda t, r_, c_: t[:, r_:r_ + HR, c_:c_ + HC]
                            steps = []
                            for r_ in range(KIND_TAPS[rk]):
                                for c_ in range(KIND_TAPS[ck]):
                                    rt, ct = KIND_AT[rk] + r_, KIND_AT[ck] + c_
                                    steps.append((wh[:, rt, ct, :], window(h, r_, c_)))
                                    steps.append((wl[:, rt, ct, :], window(h2, r_, c_)))
                            for rt, ct, rows, k in LOWS[part]:
                                steps.append((wp[0:rows, k, :], window(l[0:rows], rt - KIND_AT[rk], ct - KIND_AT[ck])))
                            if q == 0:
                                pe.wait_ge(s_h, m * 6 + 6 + START)
                                pe.wait_ge(s_ext[i], (b * (SS // 2) + m2 + 1) * EXT + START)
                                pe.wait_ge(s_m0, m + START)
                            elif q == 1:
                                pe.wait_ge(s_mid, m * SV + START)
                            elif q == 8:
                                pe.wait_ge(s_mid, m * SV + 2 + START)
                            for k, (w, src) in enumerate(steps):
                                last = mm(ps[0:C, PSBANK[part], 0:OUTS], w, src, start=k == 0, stop=k == len(steps) - 1)
                            last.then_inc(s_cv, 1)

        @block.scalar
        def _(act):
            act.wait_ge(s_pool0, NPOOL)

            def deviation(products):
                act.wait_ge(s_pst, products + START)
                act.activation(col(RSTD), ps[0:C, 7, 0:1], ACT.Sqrt, bias=epsc[0:C]).then_inc(s_sqrt, 1)

            with act.Fori(0, B) as b:
                deviation(b * NPST + 2)
                act.wait_ge(s_st, b * NST + N_AFF + START)

                def normed(t, i):
                    act.wait_ge(s_pa, b * AT + t + 1 - AD + START)
                    act.activation(y1[:, i, :], X[:, bass.ds(t * BANK + XP * W, BANK)], ACT.Identity,
                                   bias=col(SBI), scale=col(SA)).then_inc(s_y1, 1)

                def squares(t, i):
                    act.wait_ge(s_pa, b * AT + t + 1 + START)
                    act.wait_ge(s_vr, b * AT + t - 1 + START)
                    act.activation(sq[:, i % 2], ps[:, 2 * i:2 * i + 2, :].rearrange("p b (r c) -> p (b r) c", r=2)[:, :, CO:NP],
                                   ACT.Square, scale=float(C) ** -0.5).then_inc(s_sq, 1)

                def deviations(t, i):
                    act.wait_ge(s_vr, b * AT + t + 1 + START)
                    act.activation(sd[:, i, :], vr[:, i, :], ACT.Sqrt, bias=epsc[:]).then_inc(s_sd, 1)
                with act.Fori(0, 1) as t4:
                    for i in range(AD):
                        normed(t4 * AD + i, i)
                with act.Fori(0, AT // AD - 1) as t4:
                    for i in range(AD):
                        squares(t4 * AD + i, i)
                        normed(t4 * AD + AD + i, i)
                        deviations(t4 * AD + i, i)
                for i in range(AD):
                    squares(AT - AD + i, i)
                    deviations(AT - AD + i, i)
                with act.Fori(0, DK // 2) as k2:
                    for i in range(2):
                        act.wait_ge(s_dw, b * DK + k2 * 2 + i + 1 + START)
                        act.activation(Q[:, bass.ds((k2 * 2 + i) * DC, DC), :].rearrange("p (k c) h -> p k (c h)", k=2),
                                       ps[:, 4 + 2 * i:6 + 2 * i, 0:3 * H], ACT.Copy).then_inc(s_qd, 1)
                act.wait_ge(s_qd, (b + 1) * DK + START)
                with act.Fori(0, GS // 2) as g2:
                    n = b * (GS // 2) + g2
                    for i in range(2):
                        act.wait_ge(s_vt[i], n + START)
                        act.activation(vs[:, i, :, 0:KC], Q[:, QK:CO, bass.ds((g2 * 2 + i) * GR, GR)].rearrange("p c r -> p r c"),
                                       ACT.Copy).then_inc(s_vs[i], 1)
                    for i in range(2):
                        act.wait_ge(s_vt[i], n + 1 + START)
                        act.activation(vT[:, bass.ds((g2 * 2 + i) * 2 * P, 2 * P)], ps[:, 1 + i, 0:2 * P], ACT.Copy).then_inc(s_vc[i], 1)
                act.wait_ge(s_st, b * NST + N_DIAG + START)
                act.activation(col(DIAG, QK), col(DIAG, QK), ACT.Sqrt).then_inc(s_sqrt, 1)
                act.wait_ge(s_st, b * NST + N_NMX + START)
                act.activation(att[0:C, 2 * P + 32:2 * P + 32 + KC], att[0:C, 2 * P:2 * P + KC], ACT.Exp, bias=col(NMX),
                               accum_out=col(DEN)).then_inc(s_exp, 1)
                deviation(b * NPST + 6)
                act.wait_ge(s_st, (b + 1) * NST + START)

                def prepare(m, i, gate):
                    n = b * SS + m
                    act.wait_ge(s_sum, n * 2 + START)
                    act.wait_ge(s_l, n * 6 + START)
                    for lo_, hi_, bias, scale in ((0, 2, edge[:, 1, bass.ds(m, 1)], edge[:, 0, bass.ds(m, 1)]),
                                                  (2, SI - 2, col(SBI), col(SA)),
                                                  (SI - 2, SI, edge[:, 3, bass.ds(m, 1)], edge[:, 2, bass.ds(m, 1)])):
                        act.activation(y2[:, lo_:hi_, 2:2 + W],
                                       X[:, bass.ds(m * SR * W + lo_ * W, (hi_ - lo_) * W)].rearrange("p (r w) -> p r w", w=W),
                                       ACT.Identity, bias=bias, scale=scale).then_inc(s_y2, 1)
                    act.wait_ge(s_y2, n * 3 + 3 + START)
                    if gate:
                        act.wait_ge(s_cv, (n - 1) * 9 + START)
                    for dst, src in plain_views(hi[i]):
                        act.activation(dst, src, ACT.Copy).then_inc(s_h, 1)
                    act.wait_ge(s_sum, n * 2 + 2 + START)
                    for dst, src in sum_views(hi[i]):
                        act.activation(dst, src, ACT.Copy).then_inc(s_h, 1)

                def shared(m, q, dst):
                    act.wait_ge(s_cv, (b * SS + m) * 9 + q + 1 + START)
                    act.wait_ge(s_mid, (b * SS + m) * SV + START)
                    act.activation(dst, ps[0:C, PSBANK[TIME[q]], 0:OUTS], ACT.Copy, scale=col(OSC)).then_inc(s_m0, 1)
                prepare(0, 0, False)
                prepare(1, 1, False)
                with act.Fori(0, SS // 2 - 1) as m2:
                    for i in range(2):
                        shared(m2 * 2 + i, 0, mid[0])
                        prepare(m2 * 2 + 2 + i, i, True)
                for i in range(2):
                    shared(SS - 2 + i, 0, mid[0])

        @block.vector
        def _(dve):
            v = nc.vector
            setup = Steps(s_dv)

            def link(steps, ins):
                steps.done(ins)
                dve.wait_ge(steps.s, steps.value())
            dve.wait_ge(s_w, NLOADS * 16)
            dve.wait_ge(s_pool0, NPOOL)
            dve.wait_ge(s_pt, 7)
            link(setup, v.tensor_copy(wT, ps[0:C, 0, 0:CO]))
            link(setup, v.tensor_copy(pT[:], ps[0:C, 0, CO:NP]))
            link(setup, v.tensor_copy(wfT.rearrange("p b c -> p (b c)"), ps[0:C, 1, 0:4 * C]))
            link(setup, v.tensor_scalar(wTs, wT, col(LNW), None, ALU.mult))
            link(setup, v.tensor_scalar(lnbb, ident[0:C, :], 0.0, col(LNB), ALU.mult, ALU.add))
            dve.wait_ge(s_pt, 9)
            link(setup, v.tensor_copy(proj[:, 0:CO], ps[0:C, 2, 0:CO]))
            link(setup, v.tensor_copy(proj[:, CO:NP], center[:]))
            link(setup, v.tensor_copy(cbias[:], ps[:, 3, 0:CO]))
            for k in range(5):
                dve.wait_ge(s_pt, 10 + k)
                link(setup, v.tensor_copy(folded[:, k * 5 * C:(k + 1) * 5 * C], ps[0:C, (4 + k) % 8, 0:5 * C]))
            grid = folded.rearrange("p (y x c) -> p y (x c)", y=5, x=5)
            for t, (plus, minus) in enumerate(FOLD):
                dst = rfold[:, t].rearrange("p x c -> p (x c)")
                if minus is None:
                    link(setup, v.tensor_copy(dst, grid[:, plus]))
                else:
                    link(setup, v.tensor_tensor(dst, grid[:, plus], grid[:, minus], ALU.subtract))
            for t, (plus, minus) in enumerate(FOLD):
                if minus is None:
                    link(setup, v.tensor_copy(fast[:, :, t], rfold[:, :, plus]))
                else:
                    link(setup, v.tensor_tensor(fast[:, :, t], rfold[:, :, plus], rfold[:, :, minus], ALU.subtract))
            fastf = fast.rearrange("p r x c -> p (r x c)")
            link(setup, v.tensor_reduce(col(AMAX), fastf, AX.X, ALU.max, apply_absolute_value=True))
            assert setup.n == N_AMAX
            dve.wait_ge(s_pt, 15)
            link(setup, v.tensor_reduce(small[0:1, GMAX:GMAX + 1], ps[0:1, 1, 0:C], AX.X, ALU.max))
            link(setup, v.tensor_scalar(small[0:1, GMAX:GMAX + 1], small[0:1, GMAX:GMAX + 1], 1e-30, None, ALU.max))
            dve.wait_ge(s_pt, 16)
            link(setup, v.tensor_copy(col(AMAX), ps[0:C, 2, 0:1]))
            link(setup, v.tensor_scalar(col(POW).bitcast(i32), col(AMAX).bitcast(i32), 0x7F800000, None, ALU.bitwise_and))
            link(setup, v.reciprocal(col(WSC), col(POW)))
            link(setup, v.tensor_scalar(col(WSC), col(WSC), WTOP, None, ALU.mult))
            link(setup, v.tensor_scalar(col(OSC), col(POW), 1.0 / (WTOP * YSCALE), None, ALU.mult))
            whf, wlf = (a[0:C].rearrange("p r x c -> p (r x c)") for a in (wh, wl))
            link(setup, v.memset(wp[:].rearrange("p n c -> p (n c)"), 0.0))
            link(setup, v.tensor_scalar(whf, fastf, col(WSC), None, ALU.mult))
            link(setup, v.scalar_tensor_tensor(wlf, fastf, col(WSC), whf, ALU.mult, ALU.subtract))
            assert setup.n == N_SPLIT
            for k in range(3):
                link(setup, v.tensor_reduce(small[:, RES0 + k:RES0 + k + 1], res[:, k, :], AX.X, ALU.add))
            for j in range(3):
                for d in range(3):
                    r = RES0 + (d + j - 1) % 3
                    if d == 0:
                        link(setup, v.tensor_scalar(V[:, j, :], rawdw[:, :, d], small[:, r:r + 1], None, ALU.mult))
                    else:
                        link(setup, v.scalar_tensor_tensor(V[:, j, :], rawdw[:, :, d], small[:, r:r + 1], V[:, j, :],
                                                           ALU.mult, ALU.add))

            def affine(st, pst, root, tiles, scale):
                dve.wait_ge(s_bn, tiles + START)
                v.memset(col(MG), 0.0)
                link(st, v.bn_aggr(small[0:C, MEAN:MEAN + 2], stats[:].rearrange("p t s -> p (t s)")))
                dve.wait_ge(s_pst, pst + 1 + START)
                link(st, v.tensor_copy(col(MG), ps[0:C, 7, 0:1]))
                link(st, v.tensor_tensor(col(DEV), col(MEAN), col(MG), ALU.subtract))
                link(st, v.scalar_tensor_tensor(col(VG), col(DEV), col(DEV), col(VAR), ALU.mult, ALU.add))
                dve.wait_ge(s_sqrt, root + START)
                link(st, v.reciprocal(col(RSTD), col(RSTD)))
                link(st, v.tensor_scalar(col(SA), col(RSTD), scale, None, ALU.mult))
                st.done(v.scalar_tensor_tensor(col(SBI), col(MG), -1.0, col(SA), ALU.mult, ALU.mult))

            def statistics(m):
                for k in range(XL):
                    v.bn_stats(stats[:, bass.ds(m * XL + k, 1), :].rearrange("p o s -> p (o s)"),
                               X[:, bass.ds((m * XL + k) * BANK + XP * W, BANK)]).then_inc(s_bn, 1)
            for i in range(2):
                dve.wait_ge(s_x[i], SS // 2 * 16 + START)
            with dve.Fori(0, SS) as m:
                statistics(m)
            with dve.Fori(0, B) as b:
                st = Steps(s_st, b * NST + START)
                affine(st, b * NPST, b * 3 + 1, b * 2 * AT + AT, 1.0)

                def variances(t, i):
                    dve.wait_ge(s_sq, b * AT + t + 1 + START)
                    v.tensor_reduce(vr[:, i, :], sq[:, i % 2], AX.X, ALU.add).then_inc(s_vr, 1)

                def scaled(t, i):
                    n = b * AT + t
                    dve.wait_ge(s_sd, n + 1 + START)
                    v.reciprocal(rr[:, i, :], sd[:, i, :]).then_inc(s_rr, 1)
                    dve.wait_ge(s_rr, n + 1 + START)
                    dve.wait_ge(s_q, n - 1 + START)
                    v.tensor_tensor(pq[:, i % 2], ps[:, 2 * i:2 * i + 2, :].rearrange("p b (r c) -> p (b r) c", r=2)[:, :, 0:CO],
                                    rr[:, i, :].unsqueeze(2).broadcast_to([P, AR, CO]), ALU.mult).then_inc(s_pq, 1)
                variances(0, 0)
                with dve.Fori(0, AT // AD - 1) as t4:
                    for i in range(AD):
                        variances(t4 * AD + i + 1, (i + 1) % AD)
                        scaled(t4 * AD + i, i)
                for i in range(AD):
                    if i < AD - 1:
                        variances(AT - AD + i + 1, i + 1)
                    scaled(AT - AD + i, i)
                with dve.Fori(0, DK // 2) as k2:
                    for i in range(2):
                        dve.wait_ge(s_dw, b * DK + k2 * 2 + i - 1 + START)
                        dve.wait_ge(s_out, b * SS * 16 + START)
                        taps = V[:, :, bass.ds((k2 * 2 + i) * DM, DM)].rearrange("p j m -> p m j").unsqueeze(2)
                        mask = band[:].rearrange("p (i j) -> p i j", j=3).unsqueeze(1)
                        v.tensor_tensor(T[:, i].rearrange("p m (i j) -> p m i j", j=3),
                                        taps.broadcast_to([P, DM, BW // 3, 3]), mask.broadcast_to([P, DM, BW // 3, 3]),
                                        ALU.mult).then_inc(s_T, 1)
                dve.wait_ge(s_qd, (b + 1) * DK + START)
                v.memset(vs[:, :, :, KC:VP], 0.0)
                with dve.Fori(0, GS // 2) as g2:
                    for i in range(2):
                        dve.wait_ge(s_g[i], b * (GS // 2) + g2 + START)
                        v.tensor_copy(S[:, i], Q[:, 0:QK, bass.ds((g2 * 2 + i) * GR, GR)].rearrange("p c r -> p r c")).then_inc(s_S[i], 1)
                for i in range(2):
                    dve.wait_ge(s_g[i], (b + 1) * (GS // 2) + START)
                v.memset(att[:, 3 * P:4 * P], 0.0)
                v.memset(mblk, 0.0)
                link(st, v.tensor_copy(att[0:QK, 0:QK], ps[0:QK, 0, 0:QK]))
                link(st, v.tensor_tensor(att[0:QK, P:P + QK], att[0:QK, 0:QK], ident[0:QK, 0:QK], ALU.mult))
                link(st, v.tensor_reduce(col(DIAG, QK), att[0:QK, P:P + QK], AX.X, ALU.add))
                link(st, v.tensor_scalar(col(DIAG, QK), col(DIAG, QK), 1e-24, None, ALU.max))
                dve.wait_ge(s_sqrt, b * 3 + 2 + START)
                link(st, v.reciprocal(col(RN, QK), col(DIAG, QK)))
                link(st, v.tensor_scalar(att[0:QK, P:P + QK], att[0:QK, 0:QK], col(RN, QK), None, ALU.mult))
                dve.wait_ge(s_pst, b * NPST + 3 + START)
                logits = att[0:C, 2 * P:2 * P + KC]
                link(st, v.tensor_scalar(logits, ps[0:C, 3, C:QK], col(RN), col(TEMP), ALU.mult, ALU.mult))
                link(st, v.tensor_tensor(logits, logits, amask[:], ALU.add))
                link(st, v.tensor_reduce(col(NMX), logits, AX.X, ALU.max, negate=True))
                dve.wait_ge(s_exp, b + 1 + START)
                link(st, v.reciprocal(col(RDEN), col(DEN)))
                link(st, v.tensor_scalar(att[0:C, 3 * P:4 * P].rearrange("p (j c) -> p j c", j=4)[:, :, 0:KC],
                                         att[0:C, 2 * P + 32:2 * P + 32 + KC].unsqueeze(1).broadcast_to([C, 4, KC]),
                                         col(RDEN), None, ALU.mult))
                dve.wait_ge(s_pst, b * NPST + 4 + START)
                for j in range(AR):
                    st.done(v.tensor_copy(mblk[VP * j:VP * (j + 1), j, :], ps[VP * j:VP * (j + 1), 3, 0:C]))
                with dve.Fori(0, AT // 2) as t2:
                    n = b * (AT // 2) + t2
                    for i in range(2):
                        xt = X[:, bass.ds((t2 * 2 + i) * BANK + XP * W, BANK)]
                        dve.wait_ge(s_o[i], n + 1 + START)
                        v.tensor_tensor(xt, ps[0:C, 5 + i, :], xt, ALU.add).then_inc(s_x1[i], 1)
                    for i in range(2):
                        xt = X[:, bass.ds((t2 * 2 + i) * BANK + XP * W, BANK)]
                        dve.wait_ge(s_x1[i], n + 1 + START)
                        v.bn_stats(stats[:, bass.ds(t2 * 2 + i, 1), :].rearrange("p o s -> p (o s)"), xt).then_inc(s_bn, 1)
                affine(st, b * NPST + 4, b * 3 + 3, (b + 1) * 2 * AT, YSCALE)
                v.memset(y2[:, :, 0:2], 0.0)
                v.memset(y2[:, :, 2 + W:WP], 0.0)
                dve.wait_ge(s_st, st.value())
                for k in range(4):
                    st.done(v.tensor_scalar(edge[:, k, :], emask[:, k // 2, :], col(SA if k % 2 == 0 else SBI), None, ALU.mult))
                assert st.n == NST, st.n

                def sums(m):
                    n = b * SS + m
                    dve.wait_ge(s_y2, n * 3 + 3 + START)
                    dve.wait_ge(s_h, n * 6 + START)
                    v.tensor_tensor(rsum, y2[:, 1:SI - 1:2, :], y2[:, 2:SI:2, :], ALU.add).then_inc(s_rs, 1)
                    v.tensor_tensor(csum, y2[:, :, 1:WP - 1:2], y2[:, :, 2:WP:2], ALU.add).then_inc(s_sum, 1)
                    dve.wait_ge(s_rs, n + 1 + START)
                    v.tensor_tensor(rcsum, rsum[:, :, 1:WP - 1:2], rsum[:, :, 2:WP:2], ALU.add).then_inc(s_sum, 1)

                def lows(m, i, m2):
                    n = b * SS + m
                    dve.wait_ge(s_ext[1 - i], (b * (SS // 2) + m2) * EXT + START)
                    dve.wait_ge(s_sum, n * 2 + 2 + START)
                    views = zip(plain_views(low) + sum_views(low), plain_views(hi[i]) + sum_views(hi[i]))
                    for k, ((dst, src), (high, _)) in enumerate(views):
                        dve.wait_ge(s_h, n * 6 + k + 1 + START)
                        v.tensor_tensor(dst, src, high, ALU.subtract).then_inc(s_l, 1)

                def partial(m):
                    n = b * SS + m
                    quarter = ob.rearrange("p (k s j c) -> p s c k j", s=2, j=HC, c=2)
                    bank = lambda q: ps[0:C, PSBANK[TIME[q]], 0:OUTS]
                    dve.wait_ge(s_m0, n + 1 + START)
                    for c in range(2):
                        dve.wait_ge(s_cv, n * 9 + 2 + c + START)
                        v.scalar_tensor_tensor(mid[1 + c], bank(1 + c), col(OSC), mid[0], ALU.mult, ALU.add).then_inc(s_mid, 1)
                    dve.wait_ge(s_mid, n * SV + 2 + START)
                    dve.wait_ge(s_out, n * 16 + START)
                    for s_ in range(2):
                        dve.wait_ge(s_cv, n * 9 + 4 + s_ + START)
                        for c in range(2):
                            v.scalar_tensor_tensor(quarter[:, s_, c], bank(3 + s_).rearrange("p (k j) -> p k j", j=HC), col(OSC),
                                                   mid[1 + c].rearrange("p (k j) -> p k j", j=HC),
                                                   ALU.mult, ALU.add).then_inc(s_mid, 1)

                def final(m):
                    n = b * SS + m
                    quarter = ob.rearrange("p (k s j c) -> p s c k j", s=2, j=HC, c=2)
                    dve.wait_ge(s_res, n + 1 + START)
                    for s_ in range(2):
                        for c in range(2):
                            q = 5 + 2 * s_ + c
                            dve.wait_ge(s_cv, n * 9 + q + 1 + START)
                            v.scalar_tensor_tensor(quarter[:, s_, c], ps[0:C, PSBANK[TIME[q]], 0:OUTS].rearrange("p (k j) -> p k j", j=HC),
                                                   col(OSC), quarter[:, s_, c], ALU.mult, ALU.add).then_inc(s_mid, 1)

                def next_statistics(m, i, count):
                    with dve.If(b < B - 1):
                        dve.wait_ge(s_x[i], ((b + 1) * (SS // 2) + count) * 16 + START)
                        statistics(m)

                def unit_pair(m2, first):
                    for i in range(2):
                        m = m2 * 2 + i
                        partial(m)
                        sums(m + 2)
                        if not (first and i == 0):
                            next_statistics(m - 1, 1 - i, m2 + i)
                        final(m)
                        lows(m + 2, i, m2 + 1 + i)
                sums(0)
                lows(0, 0, 0)
                sums(1)
                lows(1, 1, 1)
                unit_pair(0, True)
                with dve.Fori(1, SS // 2 - 1) as m2:
                    unit_pair(m2, False)
                for i in range(2):
                    m = SS - 2 + i
                    partial(m)
                    next_statistics(m - 1, 1 - i, SS // 2 - 1 + i)
                    final(m)
                next_statistics(SS - 1, 1, SS // 2)


_INS = ['x', 'L0_conv_ln_w', 'L0_conv_ln_b', 'L0_conv_q_w', 'L0_conv_q_dw', 'L0_conv_kv_w', 'L0_conv_kv_dw',
        'L0_conv_proj_w', 'L0_conv_temperature', 'L1_conv_w1', 'L1_conv_w3', 'L1_conv_w5', 'L1_conv_wd', 'L1_conv_wf']


def kernel(**inputs):
    import numpy as _np
    import concourse.bacc as _bacc
    from concourse import mybir as _mybir
    from concourse.bass_utils import run_bass_kernel_spmd as _run

    nc = _bacc.Bacc("TRN2", target_bir_lowering=False, num_devices=1)
    arrays, args = {}, []
    for name in _INS:
        a = _np.ascontiguousarray(inputs[name])
        arrays[f"in_{name}_dram"] = a
        args.append(nc.dram_tensor(f"in_{name}_dram", a.shape, _mybir.dt.from_np(a.dtype), kind="ExternalInput").ap())
    shape = inputs['x'].shape
    args.append(nc.dram_tensor("out_0_dram", shape, _mybir.dt.float32, kind="ExternalOutput").ap())
    build_program(nc, *args)
    r = _run(nc, [arrays], core_ids=[0])
    return r.results[0]["out_0_dram"]
```

```python
from contextlib import ExitStack

import concourse.bass as bass
from concourse import mybir


def build_program(nc, x, ln_w, ln_b, q_w, q_dw, kv_w, kv_dw, proj_w, temperature, w1, w3, w5, wd, wf, out):
    f32, f16, i32 = mybir.dt.float32, mybir.dt.float16, mybir.dt.int32
    ALU = mybir.AluOpType
    ACT = mybir.ActivationFunctionType
    AX = mybir.AxisListType

    B, C, H, W = x.shape
    P = 128
    HEADS, GROUPS = 8, 32
    CG = C // GROUPS
    KV = kv_w.shape[0]
    KC = KV // 2
    HD = C // HEADS
    CO = C + KV
    QK = C + KC
    EPS = 1e-5
    BANK = 512

    AR = BANK // W
    AT = H // AR
    AD = 4
    NP = CO + C
    DC = 6
    DK = CO // DC
    DM = 3 * DC
    BW = 129
    GR = 8
    GS = H // GR
    VP = 32
    SR = 8
    SS = H // SR
    SI = SR + 4
    WP = W + 4
    TAPS = 25
    XP = 2
    XL = SR * W // BANK
    YSCALE = 64.0
    WTOP = 4096.0

    KIND_TAPS = (2, 3, 3)
    KIND_AT = (0, 2, 5)
    TERMS = (((1, None), (3, None)), ((0, None), (2, 1), (4, 3)), ((0, 1), (2, 3), (4, None)))
    FOLD = [t for kind in TERMS for t in kind]
    HR = SR // 2
    HC = W // 2
    ROWS = [HR + t - 1 for t in KIND_TAPS]
    COLS = [HC + t - 1 for t in KIND_TAPS]
    OUTS = HR * HC
    MEM = [(0, 0), (1, 0), (2, 0), (0, 1), (0, 2), (1, 1), (2, 1), (1, 2), (2, 2)]
    TIME = [(0, 0), (0, 1), (0, 2), (1, 0), (2, 0), (1, 1), (1, 2), (2, 1), (2, 2)]
    PSBANK = dict(zip(TIME, (0, 1, 2, 3, 4, 5, 6, 7, 2)))
    AT_EL, PART_END = {}, 0
    for part in MEM:
        AT_EL[part] = PART_END
        PART_END += ROWS[part[0]] * COLS[part[1]]
    WIDE = AT_EL[(0, 1)]
    PLAIN = AT_EL[(1, 1)]
    HALF = (PART_END + 1) // 2
    TWO_ROWS = [(0, True), (2, True), (4, False), (5, True), (7, False)]
    LOWS = {}
    for rk, ck in MEM:
        if ck == 0:
            LOWS[rk, ck] = [(rt, 0, P, k) for k, (rt, _) in enumerate(TWO_ROWS)
                            if KIND_AT[rk] <= rt < KIND_AT[rk] + KIND_TAPS[rk]]
        else:
            LOWS[rk, ck] = [(rt, KIND_AT[ck], 96, len(TWO_ROWS) + 8 * (ck - 1) + rt)
                            for rt in range(KIND_AT[rk], KIND_AT[rk] + KIND_TAPS[rk])]
    NLOW = len(TWO_ROWS) + 16

    ctx = ExitStack()
    with ctx:
        def sb(name, shape, dt=f32):
            return ctx.enter_context(nc.sbuf_tensor(name, shape, dt))

        START = 4
        counted = []

        def sem(name):
            counted.append(ctx.enter_context(nc.semaphore(name)))
            return counted[-1]

        def plain_sem(name):
            return ctx.enter_context(nc.semaphore(name))

        X = sb("X", [C, (H + 2 * XP) * W])
        Q = sb("Q", [P, CO, H])
        work = sb("work", [P, 6592])
        W16 = sb("W16", [P, (2 * 64 + NLOW) * C], f16)
        taps16 = lambda k: W16[:, k * 64 * C:(k + 1) * 64 * C].rearrange("p (r x c) -> p r x c", r=8, x=8)
        wh = taps16(0)
        wl = taps16(1)
        wp = W16[:, 2 * 64 * C:].rearrange("p (n c) -> p n c", c=C)
        W32 = W16[0:C].bitcast(f32)
        FOLDED_AT = (2 * 64 + NLOW) * C // 2 - 5 * 5 * C
        folded = W32[:, FOLDED_AT:].rearrange("p (y n) -> p y n", y=5)
        proj = sb("proj", [C, NP])
        V = sb("V", [P, 3, 3 * CO])
        band = sb("band", [P, BW])
        ident = sb("ident", [P, P])
        center = sb("center", [C, C])
        gmean = sb("gmean", [C, C])
        pT = sb("pT", [C, C])
        cbias = sb("cbias", [P, CO])
        stats = sb("stats", [C, AT, 6])
        small = sb("small", [P, 64])
        edge = sb("edge", [C, 4, SS])
        emask = sb("emask", [C, 2, SS])
        vr = sb("vr", [P, AD, AR])
        sd = sb("sd", [P, AD, AR])
        rr = sb("rr", [P, AD, AR])
        epsc = sb("epsc", [P, 1])
        amask = sb("amask", [C, KC])
        tsums = sb("tsums", [C, 4, AT // 2])
        ps = ctx.enter_context(nc.psum_tensor("ps", [P, 8, BANK], f32))

        sq = work[:, 0:2 * AR * C].rearrange("p (i r c) -> p i r c", i=2, r=AR)
        pq = work[:, 768:768 + 2 * AR * CO].rearrange("p (i r c) -> p i r c", i=2, r=AR)
        y1 = work[0:C, 4000:4000 + AD * BANK].rearrange("p (i n) -> p i n", i=AD)
        att = work[:, 0:4 * P]
        mblk = work[:, 4 * P:4 * P + 4 * C].rearrange("p (j c) -> p j c", j=4)
        junk = [work[0:C, a:a + BANK] for a in (900, 900 + BANK)]
        T = work[:, 1940:1940 + 2 * DM * BW].rearrange("p (i m x) -> p i m x", i=2, m=DM)
        vT = work[:, 1940:1940 + AT * P]
        S = work[:, 0:2 * GR * QK].rearrange("p (i r c) -> p i r c", i=2, r=GR)
        vs = work[:, 6040:6040 + 2 * GR * VP].rearrange("p (i r c) -> p i r c", i=2, r=GR)
        Qf = Q[:, :, :].rearrange("p c h -> p (c h)")
        halfs = lambda k: Qf[:, k * HALF:(k + 1) * HALF].bitcast(f16)
        hi = [halfs(i) for i in range(2)]
        hi2 = [halfs(2 + i) for i in range(2)]
        lo = [halfs(4 + i) for i in range(2)]
        low = halfs(6)[0:C]
        y2 = Qf[0:C, 7 * HALF:7 * HALF + SI * WP].rearrange("p (r w) -> p r w", w=WP)
        rsum = Qf[0:C, 7 * HALF + SI * WP:7 * HALF + (SI + ROWS[0]) * WP].rearrange("p (r w) -> p r w", w=WP)
        assert 7 * HALF + (SI + ROWS[0]) * WP <= CO * H
        csum = work[0:C, 0:SI * COLS[0]].rearrange("p (r w) -> p r w", w=COLS[0])
        rcsum = work[0:C, SI * COLS[0]:(SI + ROWS[0]) * COLS[0]].rearrange("p (r w) -> p r w", w=COLS[0])
        ob = work[0:C, 1920:1920 + SR * W]
        mid = [work[0:C, 4000 + i * OUTS:4000 + (i + 1) * OUTS] for i in range(3)]
        part_view = lambda t, part: t[:, AT_EL[part]:AT_EL[part] + ROWS[part[0]] * COLS[part[1]]] \
            .rearrange("p (r w) -> p r w", w=COLS[part[1]])

        def both(t, ck):
            a = AT_EL[1, ck]
            return t[:, a:a + 2 * ROWS[1] * COLS[ck]].rearrange("p (s r w) -> p s r w", s=2, w=COLS[ck])

        def plain_views(t):
            grid = y2.rearrange("p (k s) (j c) -> p c s k j", s=2, c=2)
            return [(both(t[0:C], 1 + c), grid[:, c]) for c in range(2)]

        def sum_views(t):
            grid = rsum.rearrange("p k (j c) -> p c k j", c=2)
            return [(part_view(t[0:C], (0, 1 + c)), grid[:, c]) for c in range(2)] + \
                   [(both(t[0:C], 0), csum.rearrange("p (k s) j -> p s k j", s=2)), (part_view(t[0:C], (0, 0)), rcsum)]
        raw5 = Qf[0:C, 0:2400]
        raw3 = Qf[0:C, 2400:2400 + 864]
        rawd = Qf[0:C, 3264:3264 + 864]
        raw1 = Qf[0:C, 4128:4128 + 96]
        rawf = Qf[0:C, 4224:4224 + 384]
        wfT = Qf[0:C, 4608:4608 + 384].rearrange("p (b c) -> p b c", b=4)
        rawdw = Qf[:, 7392:7392 + 9 * CO].rearrange("p (m d) -> p m d", d=3)
        turned = Qf[:, 5000:5000 + 3 * CO]
        rdiff = work[0:C, 0:4 * 5 * C].rearrange("p (k x c) -> p k x c", k=4, x=5)
        fastrow = [W32[:, a:a + 8 * C].rearrange("p (x c) -> p x c", x=8) for a in (3 * 4 * C, 64 * C)]
        qw = Qf[0:C, 8700:8700 + 96]
        kvw = Qf[0:KV, 8796:8796 + 96]
        pw = Qf[0:C, 8892:8892 + 96]
        wT = Qf[0:C, 9000:9000 + CO]
        wTs = Qf[0:C, 9150:9150 + CO]
        lnbb = Qf[0:C, 9300:9300 + P]
        res = Qf[:, 9500:9500 + 3 * 43].rearrange("p (k i) -> p k i", k=3)
        onesr = Qf[0:1, 9700:9700 + P]

        def col(i, n=C):
            return small[0:n, i:i + 1]
        LNW, LNB, TEMP, MEAN, VAR, MG, DEV, VG, RSTD, SA, SBI, AMAX, POW, WSC, OSC, DIAG, RN, NMX, DEN, RDEN, RES0 = range(21)
        GMAX, FMAX = 25, 26

        def pair(name):
            return [sem(name + "0"), sem(name + "1")]

        s_w = plain_sem("weights_loaded")
        UG = 4
        s_first = [plain_sem("first_rows_loaded%d" % k) for k in range(SS // UG)]
        s_x = pair("rows_loaded")
        s_pool0 = plain_sem("constants_made")
        s_pt = plain_sem("setup_products")
        s_dv = plain_sem("setup_vector_steps")
        s_fold = plain_sem("setup_scalar_steps")
        s_fmax = plain_sem("largest_folded_weights")
        s_V = plain_sem("depthwise_taps_turned")
        s_split = plain_sem("weight_split_steps")
        s_st = sem("image_vector_steps")
        s_pst = sem("image_products")
        s_exp = sem("softmax_exponentials")
        s_y1 = sem("normed_tile")
        s_pa = sem("projected_tile")
        s_sq = sem("squared_tile")
        s_vr = sem("variance_sum")
        s_sd = sem("deviation_of_tile")
        s_rr = sem("rstd_of_tile")
        s_sqrt = sem("square_roots")
        s_pq = sem("scaled_tile")
        s_q = sem("stored_tile")
        s_T = sem("band_matrices")
        s_dw = sem("depthwise_chunk")
        s_qd = sem("stored_chunk")
        s_S = pair("gram_strip")
        s_vs = pair("value_strip")
        s_g = pair("gram_products")
        s_vt = pair("value_transposed")
        s_vc = pair("value_copied")
        s_o = sem("attention_tile")
        s_x1 = sem("x1_tile")
        s_bn = sem("tile_statistics")
        s_xs = sem("x1_tile_sums")
        s_y2 = sem("normed_rows")
        s_rs = sem("row_sums")
        s_sum = sem("all_sums")
        s_h = sem("high_parts")
        s_l = sem("low_parts")
        s_ext = pair("parts_placed")
        s_extlo = pair("low_parts_placed")
        EXT, EXTLO = 4 * 16, 5 * 16
        NPLACES = 24
        s_cv = sem("convolved_part")
        s_m0 = sem("shared_part_copied")
        s_mid = sem("partial_outputs")
        s_res = sem("residual_added")
        s_out = sem("output_written")
        SV = 10
        s_wt = plain_sem("weights_placed")

        NLOADS = 13
        N_RES, N_AMAX, N_GMAX, N_WSC = 7, 8, 10, 14
        N_COPIES = 4
        N_TURNED = 3 * (3 + 2)
        N_SPLIT = 4 + 8 * (8 + 2) + 1
        NPOOL = 22
        N_MEAN, N_VG, N_AFF = 1, 4, 7
        N_DIAG, N_SCALED, N_NMX, N_ATT, N_MBLK = (N_AFF + k for k in (4, 6, 9, 11, 15))
        N_TILES = N_MBLK + 5
        NST, NPST = N_TILES + N_AFF + 4, 6
        block = ctx.enter_context(nc.Block())

        class Steps:
            def __init__(self, s, base=0):
                self.s, self.base, self.n = s, base, 0

            def done(self, ins):
                ins.then_inc(self.s, 1)
                self.n += 1

            def value(self):
                return self.base + self.n

        @block.sync
        def _(sync):
            loads = [
                (qw, q_w), (kvw, kv_w), (pw, proj_w),
                (raw1, w1.rearrange("m c a b -> m (c a b)")),
                (raw3, w3.rearrange("m c a b -> m (c a b)")),
                (raw5, w5.rearrange("m c a b -> m (c a b)")),
                (rawd, wd.rearrange("m c a b -> m (c a b)")),
                (rawf, wf.rearrange("m c a b -> m (c a b)")),
                (col(LNW), ln_w.rearrange("(c o) -> c o", o=1)),
                (col(LNB), ln_b.rearrange("(c o) -> c o", o=1)),
                (col(TEMP), bass.AP(tensor=temperature.tensor, offset=0, ap=[[1, HEADS], [0, HD], [1, 1]])),
                (rawdw[:, 0:3 * C, :].rearrange("p m d -> p (m d)"),
                 bass.AP(tensor=q_dw.tensor, offset=0, ap=[[0, P], [1, 9 * C]])),
                (rawdw[:, 3 * C:3 * CO, :].rearrange("p m d -> p (m d)"),
                 bass.AP(tensor=kv_dw.tensor, offset=0, ap=[[0, P], [1, 9 * KV]])),
            ]
            for s_ in counted:
                sync.sem_inc(s_, START)
            for dst, src in loads:
                sync.dma_start(dst, src).then_inc(s_w, 16)
            assert len(loads) == NLOADS
            def load_rows(image, m, loaded):
                sync.dma_start(X[:, bass.ds(m * SR * W + XP * W, SR * W)] if not isinstance(m, int) else
                               X[:, (m * SR + XP) * W:((m + 1) * SR + XP) * W],
                               x[image, :, m * SR:(m + 1) * SR, :].rearrange("o c h w -> (o c) (h w)")).then_inc(loaded, 16)
            for m in range(SS):
                load_rows(slice(0, 1), m, s_first[m // UG])
            sync.wait_ge(s_split, N_SPLIT)
            places = [(wh[C:P], wh[0:32]), (wl[C:P], wh[32:64])]
            for k, (rt, second) in enumerate(TWO_ROWS):
                for row in range(1 + second):
                    for ct in range(2):
                        q = 2 * row + ct
                        places.append((wp[32 * q:32 * q + 32, k, :], wh[64:C, rt + row, ct, :]))
            for ck in (1, 2):
                for q in range(3):
                    at = len(TWO_ROWS) + 8 * (ck - 1)
                    places.append((wp[32 * q:32 * q + 32, at:at + 8, :], wh[64:C, :, KIND_AT[ck] + q, :]))
            for dst, src in places:
                sync.dma_start(dst, src).then_inc(s_wt, 16)
            assert len(places) == NPLACES

            def place_low(b, m, i):
                for steps, start, end in ((2, PLAIN, PART_END), (6, 0, PLAIN)):
                    sync.wait_ge(s_h, (b * SS + m) * 6 + steps + START)
                    sync.dma_start(hi2[i][0:C, start:end], hi[i][0:C, start:end]).then_inc(s_ext[i], 16)
                sync.wait_ge(s_l, (b * SS + m) * 6 + 6 + START)
                copies = [(hi[i][C:P], 0, 0, 0, PART_END), (hi2[i][C:P], 32, 0, 0, PART_END),
                          (lo[i][0:32], 64, 0, 0, PART_END), (lo[i][32:64], 64, 1, 0, PART_END - 1),
                          (lo[i][64:96], 64, COLS[0], 0, WIDE), (lo[i][96:P], 64, COLS[0] + 1, 0, WIDE),
                          (lo[i][64:96], 64, 2, WIDE, PART_END - 2)]
                for k, (dst, channel, shift, start, end) in enumerate(copies):
                    sync.dma_start(dst[:, start:end], low[channel:channel + 32, start + shift:end + shift]) \
                        .then_inc(s_ext[i] if k < 2 else s_extlo[i], 16)

            with sync.Fori(0, B) as b:
                place_low(b, 0, 0)
                place_low(b, 1, 1)
                for m in range(SS):
                    i = m % 2
                    with sync.If(b < B - 1):
                        sync.wait_ge(s_res, b * SS + m + 1 + START)
                        sync.wait_ge(s_y2, (b * SS + min(m + 1, SS - 1) + 1) * 3 + START)
                        load_rows(bass.ds((b + 1) % B, 1), m, s_x[i])
                    sync.wait_ge(s_mid, (b * SS + m + 1) * SV + START)
                    sync.dma_start(out[bass.ds(b, 1), :, m * SR:(m + 1) * SR, :].rearrange("o c h w -> (o c) (h w)"),
                                   ob).then_inc(s_out, 16)
                    if m < SS - 2:
                        place_low(b, m + 2, i)
            sync.wait_ge(s_out, B * SS * 16 + START)

        @block.gpsimd
        def _(pool):
            n = [0]

            def link(ins):
                n[0] += 1
                ins.then_inc(s_pool0, 1)
                pool.wait_ge(s_pool0, n[0])
            link(pool.memset(ident[:], 0.0))
            link(pool.affine_select(out=ident[:], in_=ident[:], compare_op=ALU.not_equal, fill=1.0, base=0,
                                    pattern=[[-1, P]], channel_multiplier=1))
            link(pool.memset(center[:], -1.0 / C))
            link(pool.affine_select(out=center[:], in_=center[:], compare_op=ALU.not_equal, fill=1.0 - 1.0 / C, base=0,
                                    pattern=[[-1, C]], channel_multiplier=1))
            g3 = gmean[:].rearrange("p (g k) -> p g k", k=CG)
            link(pool.memset(gmean[:], 1.0 / CG))
            link(pool.affine_select(out=g3, in_=g3, compare_op=ALU.is_ge, fill=0.0, base=0,
                                    pattern=[[-CG, GROUPS], [0, CG]], channel_multiplier=1))
            link(pool.affine_select(out=g3, in_=g3, compare_op=ALU.is_ge, fill=0.0, base=CG - 1,
                                    pattern=[[CG, GROUPS], [0, CG]], channel_multiplier=-1))
            link(pool.memset(band[:], 1.0))
            link(pool.affine_select(out=band[:], in_=band[:], compare_op=ALU.is_ge, fill=0.0, base=1,
                                    pattern=[[-1, BW]], channel_multiplier=1))
            link(pool.affine_select(out=band[:], in_=band[:], compare_op=ALU.is_ge, fill=0.0, base=1,
                                    pattern=[[1, BW]], channel_multiplier=-1))
            link(pool.memset(res, 0.0))
            link(pool.affine_select(out=res, in_=res, compare_op=ALU.not_equal, fill=1.0, base=0,
                                    pattern=[[-1, 3], [-3, 43]], channel_multiplier=1))
            m3 = amask[:].rearrange("p (g k) -> p g k", g=2)
            link(pool.memset(amask[:], 0.0))
            link(pool.affine_select(out=m3[:, 0, :], in_=m3[:, 0, :], compare_op=ALU.is_ge, fill=-1e30, base=C // 2 - 1,
                                    pattern=[[0, KC // 2]], channel_multiplier=-1))
            link(pool.affine_select(out=m3[:, 1, :], in_=m3[:, 1, :], compare_op=ALU.is_ge, fill=-1e30, base=-(C // 2),
                                    pattern=[[0, KC // 2]], channel_multiplier=1))
            link(pool.memset(emask[:], 1.0))
            link(pool.memset(emask[:, 0, 0:1], 0.0))
            link(pool.memset(emask[:, 1, SS - 1:SS], 0.0))
            link(pool.memset(onesr, 1.0))
            link(pool.memset(X[:, 0:XP * W], 0.0))
            link(pool.memset(X[:, (XP + H) * W:], 0.0))
            link(pool.memset(epsc[:], EPS))
            assert n[0] == NPOOL
            pool.wait_ge(s_w, NLOADS * 16)
            pool.wait_ge(s_dv, N_RES)
            turning = Steps(s_V)
            for j in range(3):
                for d in range(3):
                    at = RES0 + (d + j - 1) % 3
                    turn = small[:, at:at + 1]
                    product = turned if d else V[:, j, :]
                    turning.done(pool.tensor_scalar(product, rawdw[:, :, d], turn, None, ALU.mult))
                    pool.wait_ge(s_V, turning.value())
                    if d:
                        turning.done(pool.tensor_tensor(V[:, j, :], V[:, j, :], turned, ALU.add))
                        pool.wait_ge(s_V, turning.value())
            assert turning.n == N_TURNED

            def split_weights():
                split = Steps(s_split)

                def step(ins):
                    split.done(ins)
                    pool.wait_ge(s_split, split.value())
                pool.wait_ge(s_fold, N_COPIES + 5)
                rows = {}
                for t, (plus, minus) in enumerate(FOLD):
                    if minus is None:
                        rows[t] = folded[:, plus].rearrange("p (x c) -> p x c", x=5)
                for k, t in enumerate(t for t in range(8) if t not in rows):
                    plus, minus = FOLD[t]
                    rows[t] = rdiff[:, k]
                    step(pool.tensor_tensor(rdiff[:, k].rearrange("p x c -> p (x c)"), folded[:, plus], folded[:, minus],
                                            ALU.subtract))
                plain = [t for t in range(8) if FOLD[t][1] is None]
                for k, t in enumerate(plain + [t for t in range(8) if t not in plain]):
                    fast = fastrow[k // 4]
                    for ct, (plus, minus) in enumerate(FOLD):
                        if minus is None:
                            step(pool.tensor_copy(fast[:, ct], rows[t][:, plus]))
                        else:
                            step(pool.tensor_tensor(fast[:, ct], rows[t][:, plus], rows[t][:, minus], ALU.subtract))
                    step(pool.tensor_copy(wh[0:C, t], fast))
                    step(pool.tensor_tensor(wl[0:C, t], fast, wh[0:C, t], ALU.subtract))
                step(pool.memset(wp.rearrange("p n c -> p (n c)"), 0.0))
                assert split.n == N_SPLIT

            with pool.Fori(0, B) as b:
                with pool.Fori(0, AT // 2) as t2:
                    for i in range(2):
                        pool.wait_ge(s_pq, b * AT + t2 * 2 + i + 1 + START)
                        pool.tensor_tensor(Q[:, :, bass.ds((t2 * 2 + i) * AR, AR)].rearrange("p c r -> p r c"), pq[:, i],
                                           cbias[:].unsqueeze(1).broadcast_to([P, AR, CO]), ALU.add).then_inc(s_q, 1)
                with pool.If(b < 1):
                    pool.wait_ge(s_q, AT + START)
                    split_weights()
                with pool.Fori(0, SS) as m:
                    pool.wait_ge(s_mid, (b * SS + m) * SV + 6 + START)
                    pool.tensor_tensor(ob, ob, X[:, bass.ds(m * SR * W + XP * W, SR * W)], ALU.add).then_inc(s_res, 1)

        @block.tensor
        def _(pe):
            setup = Steps(s_pt)
            mm, tr = nc.tensor.matmul, nc.tensor.transpose
            idc = ident[0:C, 0:C]
            pe.wait_ge(s_w, NLOADS * 16)
            pe.wait_ge(s_pool0, NPOOL)
            setup.done(tr(ps[0:C, 0, 0:C], qw, idc))
            setup.done(tr(ps[0:C, 0, C:CO], kvw, ident[0:KV, 0:KV]))
            setup.done(tr(ps[0:C, 0, CO:NP], pw, idc))
            for k in range(4):
                setup.done(tr(ps[0:C, 1, k * C:(k + 1) * C], rawf[:, k * C:(k + 1) * C], idc))
            pe.wait_ge(s_dv, 4)
            setup.done(mm(ps[0:C, 2, 0:CO], center[:], wTs, start=True, stop=True))
            setup.done(mm(ps[:, 3, 0:CO], lnbb, wT, start=True, stop=True))
            k3, k5, kd = (a.rearrange("m (c t) -> m c t", c=C) for a in (raw3, raw5, rawd))
            for t in range(TAPS):
                if t == 20:
                    pe.wait_ge(s_fold, 1)
                dy, dx = divmod(t, 5)
                terms = [(k5[:, :, t], 2)]
                if 1 <= dy <= 3 and 1 <= dx <= 3:
                    terms.append((k3[:, :, (dy - 1) * 3 + dx - 1], 1))
                if dy % 2 == 0 and dx % 2 == 0:
                    terms.append((kd[:, :, dy // 2 * 3 + dx // 2], 3))
                if t == TAPS // 2:
                    terms.append((raw1, 0))
                for m, (w, br) in enumerate(terms):
                    last = mm(ps[0:C, (4 + t // 5) % 8, t % 5 * C:(t % 5 + 1) * C], w, wfT[:, br, :],
                              start=m == 0, stop=m == len(terms) - 1)
                if t % 5 == 4:
                    setup.done(last)
            pe.wait_ge(s_dv, N_AMAX)
            setup.done(tr(ps[0:1, 1, 0:C], col(AMAX), idc))
            pe.wait_ge(s_dv, N_GMAX)
            pe.wait_ge(s_fold, N_COPIES)
            setup.done(mm(ps[0:C, 2, 0:1], onesr[0:1, 0:C], small[0:1, GMAX:GMAX + 1], start=True, stop=True))

            pe.wait_ge(s_fold, N_COPIES + 5)

            def keep_warm(bank, count):
                for _ in range(count):
                    mm(ps[:, bank, 0:P], ident[:], ident[:], start=True, stop=True)

            def group_means(st, first):
                pe.wait_ge(s_st, first + N_MEAN + START)
                st.done(mm(ps[0:C, 7, 0:1], gmean[:], col(MEAN), start=True, stop=True))
                keep_warm(0, 4)
                pe.wait_ge(s_st, first + N_VG + START)
                st.done(mm(ps[0:C, 7, 0:1], gmean[:], col(VG), start=True, stop=True))

            with pe.Fori(0, B) as b:
                st = Steps(s_pst, b * NPST)
                pe.wait_ge(s_m0, b * SS + START)
                keep_warm(0, 12)
                group_means(st, b * NST)
                keep_warm(0, 9)
                with pe.Fori(0, AT // AD) as t4:
                    for i in range(AD):
                        n = b * AT + t4 * AD + i
                        pe.wait_ge(s_y1, n + 1 + START)
                        pe.wait_ge(s_pq, n + 1 - AD + START)
                        for r in range(AR):
                            last = mm(ps[:, 2 * i + r // 2, r % 2 * 256:r % 2 * 256 + NP], y1[:, i, r * W:(r + 1) * W],
                                      proj[:], start=True, stop=True)
                        last.then_inc(s_pa, 1)
                pe.wait_ge(s_pq, b * AT + AT - AD + 1 + START)
                keep_warm(0, 27)
                with pe.Fori(0, DK // 2) as k2:
                    for i in range(2):
                        n = b * DK + k2 * 2 + i
                        pe.wait_ge(s_q, (b + 1) * AT + START)
                        pe.wait_ge(s_T, n + 1 + START)
                        pe.wait_ge(s_qd, n - 1 + START)
                        for c in range(DC):
                            o = ps[:, 4 + 2 * i + c // 3, c % 3 * H:(c % 3 + 1) * H]
                            src = Q[:, bass.ds((k2 * 2 + i) * DC + c, 1), :].rearrange("p o h -> p (o h)")
                            mm(o, T[:, i, 3 * c + 1, 0:W], src, start=True, stop=False)
                            mm(o[:, 1:H], T[:, i, 3 * c, 0:W], src[:, 0:H - 1], start=False, stop=False)
                            last = mm(o[:, 0:H - 1], T[:, i, 3 * c + 2, 0:W], src[:, 1:H], start=False, stop=True)
                        last.then_inc(s_dw, 1)

                def gram(g2, first):
                    for i in range(2):
                        n = b * (GS // 2) + g2
                        pe.wait_ge(s_S[i], n + 1 + START)
                        for r in range(GR):
                            last = mm(ps[0:QK, 0, 0:QK], S[:, i, r, :], S[:, i, r, :],
                                      start=first and i == 0 and r == 0, stop=True, skip_group_check=True)
                        last.then_inc(s_g[i], 1)
                        pe.wait_ge(s_vs[i], n + 1 + START)
                        pe.wait_ge(s_vc[i], n + START)
                        for j in range(GR // 4):
                            last = tr(ps[:, 1 + i, j * P:(j + 1) * P],
                                      vs[:, i, 4 * j:4 * j + 4, :].rearrange("p r c -> p (r c)"), ident[:])
                        last.then_inc(s_vt[i], 1)
                gram(0, True)
                with pe.Fori(1, GS // 2) as g2:
                    gram(g2, False)
                keep_warm(4, 7)
                pe.wait_ge(s_st, b * NST + N_SCALED + START)
                st.done(tr(ps[0:QK, 3, 0:QK], att[0:QK, P:P + QK], ident[0:QK, 0:QK]))
                keep_warm(4, 5)
                pe.wait_ge(s_st, b * NST + N_ATT + START)
                st.done(mm(ps[:, 3, 0:C], att[0:C, 3 * P:4 * P], pT[:], start=True, stop=True))
                keep_warm(4, 4)
                with pe.Fori(0, AT // AD) as t4:
                    for i in range(AD):
                        for j in range(2):
                            pe.wait_ge(s_vc[j], (b + 1) * (GS // 2) + START)
                        pe.wait_ge(s_st, b * NST + N_MBLK + START)
                        pe.wait_ge(s_x1, b * AT + t4 * AD + i + 1 - AD + START)
                        for j in range(AR):
                            last = mm(ps[0:C, 4 + i, j * W:(j + 1) * W], mblk[:, j, :],
                                      vT[:, bass.ds((t4 * AD + i) * P, P)], start=True, stop=True)
                        last.then_inc(s_o, 1)
                keep_warm(0, 22)
                group_means(st, b * NST + N_TILES)
                keep_warm(0, 64)
                assert st.n == NPST
                with pe.Fori(0, SS // 2) as m2:
                    for i in range(2):
                        m = b * SS + m2 * 2 + i
                        for q, part in enumerate(TIME):
                            rk, ck = part
                            h, h2, l = (part_view(t[i], part) for t in (hi, hi2, lo))
                            window = lambda t, r_, c_: t[:, r_:r_ + HR, c_:c_ + HC]
                            steps = []
                            for r_ in range(KIND_TAPS[rk]):
                                for c_ in range(KIND_TAPS[ck]):
                                    rt, ct = KIND_AT[rk] + r_, KIND_AT[ck] + c_
                                    steps.append((wh[:, rt, ct, :], window(h, r_, c_)))
                                    steps.append((wl[:, rt, ct, :], window(h2, r_, c_)))
                            for rt, ct, rows, k in LOWS[part]:
                                steps.append((wp[0:rows, k, :], window(l[0:rows], rt - KIND_AT[rk], ct - KIND_AT[ck])))
                            if q == 0:
                                pe.wait_ge(s_wt, NPLACES * 16)
                                pe.wait_ge(s_h, m * 6 + 6 + START)
                                pe.wait_ge(s_ext[i], (b * (SS // 2) + m2 + 1) * EXT + START)
                                pe.wait_ge(s_m0, m + START)
                            elif q == 1:
                                pe.wait_ge(s_mid, m * SV + START)
                            elif q == 8:
                                pe.wait_ge(s_mid, m * SV + 2 + START)
                            for k, (w, src) in enumerate(steps):
                                if q == 0 and k == len(steps) - len(LOWS[part]):
                                    pe.wait_ge(s_extlo[i], (b * (SS // 2) + m2 + 1) * EXTLO + START)
                                last = mm(ps[0:C, PSBANK[part], 0:OUTS], w, src, start=k == 0, stop=k == len(steps) - 1)
                            last.then_inc(s_cv, 1)

        @block.scalar
        def _(act):
            act.wait_ge(s_pool0, NPOOL)
            act.wait_ge(s_pt, 7)
            act.wait_ge(s_dv, 1)
            act.activation(pT[:], ps[0:C, 0, CO:NP], ACT.Copy).then_inc(s_fold, 1)
            act.activation(proj[:, CO:NP], center[:], ACT.Copy).then_inc(s_fold, 1)
            act.wait_ge(s_pt, 9)
            act.activation(proj[:, 0:CO], ps[0:C, 2, 0:CO], ACT.Copy).then_inc(s_fold, 1)
            act.activation(cbias[:], ps[:, 3, 0:CO], ACT.Copy).then_inc(s_fold, 1)
            act.wait_ge(s_dv, N_WSC)
            for k in range(5):
                act.activation(folded[:, k], ps[0:C, (4 + k) % 8, 0:5 * C], ACT.Copy, scale=col(WSC)).then_inc(s_fold, 1)

            def deviation(products):
                act.wait_ge(s_pst, products + START)
                act.activation(col(RSTD), ps[0:C, 7, 0:1], ACT.Sqrt, bias=epsc[0:C]).then_inc(s_sqrt, 1)

            with act.Fori(0, B) as b:
                deviation(b * NPST + 2)
                act.wait_ge(s_st, b * NST + N_AFF + START)

                def normed(t, i):
                    act.wait_ge(s_pa, b * AT + t + 1 - AD + START)
                    act.activation(y1[:, i, :], X[:, bass.ds(t * BANK + XP * W, BANK)], ACT.Identity,
                                   bias=col(SBI), scale=col(SA)).then_inc(s_y1, 1)

                def squares(t, i):
                    act.wait_ge(s_pa, b * AT + t + 1 + START)
                    act.wait_ge(s_vr, b * AT + t - 1 + START)
                    act.activation(sq[:, i % 2], ps[:, 2 * i:2 * i + 2, :].rearrange("p b (r c) -> p (b r) c", r=2)[:, :, CO:NP],
                                   ACT.Square, scale=float(C) ** -0.5).then_inc(s_sq, 1)

                def deviations(t, i):
                    act.wait_ge(s_vr, b * AT + t + 1 + START)
                    act.activation(sd[:, i, :], vr[:, i, :], ACT.Sqrt, bias=epsc[:]).then_inc(s_sd, 1)
                with act.Fori(0, 1) as t4:
                    for i in range(AD):
                        normed(t4 * AD + i, i)
                with act.Fori(0, AT // AD - 1) as t4:
                    for i in range(AD):
                        squares(t4 * AD + i, i)
                        normed(t4 * AD + AD + i, i)
                        deviations(t4 * AD + i, i)
                for i in range(AD):
                    squares(AT - AD + i, i)
                    deviations(AT - AD + i, i)
                with act.Fori(0, DK // 2) as k2:
                    for i in range(2):
                        act.wait_ge(s_dw, b * DK + k2 * 2 + i + 1 + START)
                        act.activation(Q[:, bass.ds((k2 * 2 + i) * DC, DC), :].rearrange("p (k c) h -> p k (c h)", k=2),
                                       ps[:, 4 + 2 * i:6 + 2 * i, 0:3 * H], ACT.Copy).then_inc(s_qd, 1)
                act.wait_ge(s_qd, (b + 1) * DK + START)
                with act.Fori(0, GS // 2) as g2:
                    n = b * (GS // 2) + g2
                    for i in range(2):
                        act.wait_ge(s_vt[i], n + START)
                        act.activation(vs[:, i, :, 0:KC], Q[:, QK:CO, bass.ds((g2 * 2 + i) * GR, GR)].rearrange("p c r -> p r c"),
                                       ACT.Copy).then_inc(s_vs[i], 1)
                    for i in range(2):
                        act.wait_ge(s_vt[i], n + 1 + START)
                        act.activation(vT[:, bass.ds((g2 * 2 + i) * 2 * P, 2 * P)], ps[:, 1 + i, 0:2 * P], ACT.Copy).then_inc(s_vc[i], 1)
                act.wait_ge(s_st, b * NST + N_DIAG + START)
                act.activation(col(DIAG, QK), col(DIAG, QK), ACT.Sqrt).then_inc(s_sqrt, 1)
                act.wait_ge(s_st, b * NST + N_NMX + START)
                act.activation(att[0:C, 2 * P + 32:2 * P + 32 + KC], att[0:C, 2 * P:2 * P + KC], ACT.Exp, bias=col(NMX),
                               accum_out=col(DEN)).then_inc(s_exp, 1)
                with act.Fori(0, AT // 2) as t2:
                    act.wait_ge(s_x1, b * AT + t2 * 2 + 1 + START)
                    xt = X[:, bass.ds(t2 * 2 * BANK + XP * W, BANK)]
                    act.wait_ge(s_xs, (b * (AT // 2) + t2) * 2 - 1 + START)
                    act.activation(junk[0], xt, ACT.Copy, scale=1.0 / BANK,
                                   accum_out=tsums[:, 0, bass.ds(t2, 1)]).then_inc(s_xs, 1)
                    act.wait_ge(s_xs, (b * (AT // 2) + t2) * 2 + START)
                    act.activation(junk[1], xt, ACT.Square, bias=col(MEAN), scale=-1.0,
                                   accum_out=tsums[:, 1, bass.ds(t2, 1)]).then_inc(s_xs, 1)
                deviation(b * NPST + 6)

                def prepare(m, i, gate):
                    n = b * SS + m
                    act.wait_ge(s_sum, n * 2 + START)
                    act.wait_ge(s_l, n * 6 + START)
                    act.wait_ge(s_st, b * NST + N_TILES + N_AFF + START)
                    for lo_, hi_, bias, scale in ((2, SI - 2, col(SBI), col(SA)),
                                                  (0, 2, edge[:, 1, bass.ds(m, 1)], edge[:, 0, bass.ds(m, 1)]),
                                                  (SI - 2, SI, edge[:, 3, bass.ds(m, 1)], edge[:, 2, bass.ds(m, 1)])):
                        if lo_ == 0:
                            act.wait_ge(s_st, (b + 1) * NST + START)
                        act.activation(y2[:, lo_:hi_, 2:2 + W],
                                       X[:, bass.ds(m * SR * W + lo_ * W, (hi_ - lo_) * W)].rearrange("p (r w) -> p r w", w=W),
                                       ACT.Identity, bias=bias, scale=scale).then_inc(s_y2, 1)
                    act.wait_ge(s_y2, n * 3 + 3 + START)
                    if gate:
                        act.wait_ge(s_cv, (n - 1) * 9 + START)
                    for dst, src in plain_views(hi[i]):
                        act.activation(dst, src, ACT.Copy).then_inc(s_h, 1)
                    act.wait_ge(s_sum, n * 2 + 2 + START)
                    for dst, src in sum_views(hi[i]):
                        act.activation(dst, src, ACT.Copy).then_inc(s_h, 1)

                def shared(m, q, dst):
                    act.wait_ge(s_cv, (b * SS + m) * 9 + q + 1 + START)
                    act.wait_ge(s_mid, (b * SS + m) * SV + START)
                    act.activation(dst, ps[0:C, PSBANK[TIME[q]], 0:OUTS], ACT.Copy, scale=col(OSC)).then_inc(s_m0, 1)
                prepare(0, 0, False)
                prepare(1, 1, False)
                with act.Fori(0, SS // 2 - 1) as m2:
                    for i in range(2):
                        shared(m2 * 2 + i, 0, mid[0])
                        prepare(m2 * 2 + 2 + i, i, True)
                for i in range(2):
                    shared(SS - 2 + i, 0, mid[0])

        @block.vector
        def _(dve):
            v = nc.vector
            setup = Steps(s_dv)

            def link(steps, ins):
                steps.done(ins)
                dve.wait_ge(steps.s, steps.value())
            dve.wait_ge(s_w, NLOADS * 16)
            dve.wait_ge(s_pool0, NPOOL)
            dve.wait_ge(s_pt, 7)
            link(setup, v.tensor_copy(wT, ps[0:C, 0, 0:CO]))
            link(setup, v.tensor_copy(wfT.rearrange("p b c -> p (b c)"), ps[0:C, 1, 0:4 * C]))
            link(setup, v.tensor_scalar(wTs, wT, col(LNW), None, ALU.mult))
            link(setup, v.tensor_scalar(lnbb, ident[0:C, :], 0.0, col(LNB), ALU.mult, ALU.add))
            for k in range(3):
                link(setup, v.tensor_reduce(small[:, RES0 + k:RES0 + k + 1], res[:, k, :], AX.X, ALU.add))
            assert setup.n == N_RES

            def statistics(m):
                for k in range(XL):
                    v.bn_stats(stats[:, bass.ds(m * XL + k, 1), :].rearrange("p o s -> p (o s)"),
                               X[:, bass.ds((m * XL + k) * BANK + XP * W, BANK)]).then_inc(s_bn, 1)
            def first_statistics(k):
                dve.wait_ge(s_first[k], UG * 16)
                with dve.Fori(k * UG, (k + 1) * UG) as m:
                    statistics(m)
            for k in range(SS // UG - 1):
                first_statistics(k)
            dve.wait_ge(s_pt, 14)
            for k in range(5):
                v.tensor_reduce(small[0:C, FMAX + k:FMAX + k + 1], ps[0:C, (4 + k) % 8, 0:5 * C], AX.X, ALU.max,
                                apply_absolute_value=True).then_inc(s_fmax, 1)
            dve.wait_ge(s_fmax, 5)
            link(setup, v.tensor_reduce(col(AMAX), small[0:C, FMAX:FMAX + 5], AX.X, ALU.max))
            assert setup.n == N_AMAX
            dve.wait_ge(s_pt, 15)
            link(setup, v.tensor_reduce(small[0:1, GMAX:GMAX + 1], ps[0:1, 1, 0:C], AX.X, ALU.max))
            link(setup, v.tensor_scalar(small[0:1, GMAX:GMAX + 1], small[0:1, GMAX:GMAX + 1], 1e-30, None, ALU.max))
            assert setup.n == N_GMAX
            dve.wait_ge(s_pt, 16)
            link(setup, v.tensor_copy(col(AMAX), ps[0:C, 2, 0:1]))
            link(setup, v.tensor_scalar(col(POW).bitcast(i32), col(AMAX).bitcast(i32), 0x7F800000, None, ALU.bitwise_and))
            link(setup, v.reciprocal(col(WSC), col(POW)))
            link(setup, v.tensor_scalar(col(WSC), col(WSC), WTOP, None, ALU.mult))
            assert setup.n == N_WSC
            link(setup, v.tensor_scalar(col(OSC), col(POW), 1.0 / (WTOP * YSCALE), None, ALU.mult))
            first_statistics(SS // UG - 1)

            def affine(st, pst, root, tiles, scale):
                dve.wait_ge(s_bn, tiles + START)
                v.memset(col(MG), 0.0)
                link(st, v.bn_aggr(small[0:C, MEAN:MEAN + 2], stats[:].rearrange("p t s -> p (t s)")))
                dve.wait_ge(s_pst, pst + 1 + START)
                link(st, v.tensor_copy(col(MG), ps[0:C, 7, 0:1]))
                link(st, v.tensor_tensor(col(DEV), col(MEAN), col(MG), ALU.subtract))
                link(st, v.scalar_tensor_tensor(col(VG), col(DEV), col(DEV), col(VAR), ALU.mult, ALU.add))
                dve.wait_ge(s_sqrt, root + START)
                link(st, v.reciprocal(col(RSTD), col(RSTD)))
                link(st, v.tensor_scalar(col(SA), col(RSTD), scale, None, ALU.mult))
                st.done(v.scalar_tensor_tensor(col(SBI), col(MG), -1.0, col(SA), ALU.mult, ALU.mult))

            with dve.Fori(0, B) as b:
                st = Steps(s_st, b * NST + START)
                affine(st, b * NPST, b * 3 + 1, b * 3 * AT // 2 + AT, 1.0)

                def variances(t, i):
                    dve.wait_ge(s_sq, b * AT + t + 1 + START)
                    v.tensor_reduce(vr[:, i, :], sq[:, i % 2], AX.X, ALU.add).then_inc(s_vr, 1)

                def scaled(t, i):
                    n = b * AT + t
                    dve.wait_ge(s_sd, n + 1 + START)
                    v.reciprocal(rr[:, i, :], sd[:, i, :]).then_inc(s_rr, 1)
                    dve.wait_ge(s_rr, n + 1 + START)
                    dve.wait_ge(s_q, n - 1 + START)
                    v.tensor_tensor(pq[:, i % 2], ps[:, 2 * i:2 * i + 2, :].rearrange("p b (r c) -> p (b r) c", r=2)[:, :, 0:CO],
                                    rr[:, i, :].unsqueeze(2).broadcast_to([P, AR, CO]), ALU.mult).then_inc(s_pq, 1)
                variances(0, 0)
                with dve.Fori(0, AT // AD - 1) as t4:
                    for i in range(AD):
                        variances(t4 * AD + i + 1, (i + 1) % AD)
                        scaled(t4 * AD + i, i)
                for i in range(AD):
                    if i < AD - 1:
                        variances(AT - AD + i + 1, i + 1)
                    scaled(AT - AD + i, i)
                with dve.Fori(0, DK // 2) as k2:
                    for i in range(2):
                        dve.wait_ge(s_dw, b * DK + k2 * 2 + i - 1 + START)
                        dve.wait_ge(s_out, b * SS * 16 + START)
                        dve.wait_ge(s_V, N_TURNED)
                        taps = V[:, :, bass.ds((k2 * 2 + i) * DM, DM)].rearrange("p j m -> p m j").unsqueeze(2)
                        mask = band[:].rearrange("p (i j) -> p i j", j=3).unsqueeze(1)
                        v.tensor_tensor(T[:, i].rearrange("p m (i j) -> p m i j", j=3),
                                        taps.broadcast_to([P, DM, BW // 3, 3]), mask.broadcast_to([P, DM, BW // 3, 3]),
                                        ALU.mult).then_inc(s_T, 1)
                dve.wait_ge(s_qd, (b + 1) * DK + START)
                dve.wait_ge(s_split, N_SPLIT)
                v.memset(vs[:, :, :, KC:VP], 0.0)
                with dve.Fori(0, GS // 2) as g2:
                    for i in range(2):
                        dve.wait_ge(s_g[i], b * (GS // 2) + g2 + START)
                        v.tensor_copy(S[:, i], Q[:, 0:QK, bass.ds((g2 * 2 + i) * GR, GR)].rearrange("p c r -> p r c")).then_inc(s_S[i], 1)
                dve.wait_ge(s_g[0], (b + 1) * (GS // 2) + START)
                v.memset(att[:, 3 * P:4 * P], 0.0)
                v.memset(mblk, 0.0)
                dve.wait_ge(s_g[1], (b + 1) * (GS // 2) + START)
                link(st, v.tensor_copy(att[0:QK, 0:QK], ps[0:QK, 0, 0:QK]))
                link(st, v.tensor_tensor(att[0:QK, P:P + QK], att[0:QK, 0:QK], ident[0:QK, 0:QK], ALU.mult))
                link(st, v.tensor_reduce(col(DIAG, QK), att[0:QK, P:P + QK], AX.X, ALU.add))
                link(st, v.tensor_scalar(col(DIAG, QK), col(DIAG, QK), 1e-24, None, ALU.max))
                dve.wait_ge(s_sqrt, b * 3 + 2 + START)
                link(st, v.reciprocal(col(RN, QK), col(DIAG, QK)))
                link(st, v.tensor_scalar(att[0:QK, P:P + QK], att[0:QK, 0:QK], col(RN, QK), None, ALU.mult))
                dve.wait_ge(s_pst, b * NPST + 3 + START)
                logits = att[0:C, 2 * P:2 * P + KC]
                link(st, v.tensor_scalar(logits, ps[0:C, 3, C:QK], col(RN), col(TEMP), ALU.mult, ALU.mult))
                link(st, v.tensor_tensor(logits, logits, amask[:], ALU.add))
                link(st, v.tensor_reduce(col(NMX), logits, AX.X, ALU.max, negate=True))
                dve.wait_ge(s_exp, b + 1 + START)
                link(st, v.reciprocal(col(RDEN), col(DEN)))
                link(st, v.tensor_scalar(att[0:C, 3 * P:4 * P].rearrange("p (j c) -> p j c", j=4)[:, :, 0:KC],
                                         att[0:C, 2 * P + 32:2 * P + 32 + KC].unsqueeze(1).broadcast_to([C, 4, KC]),
                                         col(RDEN), None, ALU.mult))
                dve.wait_ge(s_pst, b * NPST + 4 + START)
                for j in range(AR):
                    st.done(v.tensor_copy(mblk[VP * j:VP * (j + 1), j, :], ps[VP * j:VP * (j + 1), 3, 0:C]))
                with dve.Fori(0, AT // AD) as t4:
                    for i in range(AD):
                        t = t4 * AD + i
                        xt = X[:, bass.ds(t * BANK + XP * W, BANK)]
                        dve.wait_ge(s_o, b * AT + t + 1 + START)
                        v.tensor_tensor(xt, ps[0:C, 4 + i, :], xt, ALU.add).then_inc(s_x1, 1)
                        if i % 2 == 1:
                            dve.wait_ge(s_x1, b * AT + t + 1 + START)
                            v.bn_stats(stats[:, bass.ds(t, 1), :].rearrange("p o s -> p (o s)"), xt).then_inc(s_bn, 1)
                even = stats[:].rearrange("p (t s) (h f) -> p s f t h", s=2, h=2)[:, 0]
                twice = lambda a: a.unsqueeze(2).broadcast_to([C, AT // 2, 2])
                v.memset(y2[:, :, 0:2], 0.0)
                v.memset(y2[:, :, 2 + W:WP], 0.0)
                dve.wait_ge(s_xs, (b + 1) * AT + START)
                v.memset(col(MG), 0.0)
                link(st, v.tensor_copy(even[:, 1], twice(tsums[:, 0])))
                link(st, v.tensor_scalar(tsums[:, 2], tsums[:, 0], col(MEAN), None, ALU.subtract))
                link(st, v.scalar_tensor_tensor(tsums[:, 3], tsums[:, 2], -float(BANK), tsums[:, 2], ALU.mult, ALU.mult))
                link(st, v.tensor_tensor(tsums[:, 3], tsums[:, 3], tsums[:, 1], ALU.add))
                link(st, v.tensor_scalar(even[:, 2], twice(tsums[:, 3]), 0.5, None, ALU.mult))
                affine(st, b * NPST + 4, b * 3 + 3, (b + 1) * 3 * AT // 2, YSCALE)
                dve.wait_ge(s_st, st.value())
                for k in range(4):
                    st.done(v.tensor_scalar(edge[:, k, :], emask[:, k // 2, :], col(SA if k % 2 == 0 else SBI), None, ALU.mult))
                assert st.n == NST, st.n

                def sums(m):
                    n = b * SS + m
                    dve.wait_ge(s_y2, n * 3 + 3 + START)
                    dve.wait_ge(s_h, n * 6 + START)
                    v.tensor_tensor(rsum, y2[:, 1:SI - 1:2, :], y2[:, 2:SI:2, :], ALU.add).then_inc(s_rs, 1)
                    v.tensor_tensor(csum, y2[:, :, 1:WP - 1:2], y2[:, :, 2:WP:2], ALU.add).then_inc(s_sum, 1)
                    dve.wait_ge(s_rs, n + 1 + START)
                    v.tensor_tensor(rcsum, rsum[:, :, 1:WP - 1:2], rsum[:, :, 2:WP:2], ALU.add).then_inc(s_sum, 1)

                def lows(m, i, m2):
                    n = b * SS + m
                    dve.wait_ge(s_ext[1 - i], (b * (SS // 2) + m2) * EXT + START)
                    dve.wait_ge(s_extlo[1 - i], (b * (SS // 2) + m2) * EXTLO + START)
                    dve.wait_ge(s_sum, n * 2 + 2 + START)
                    views = zip(plain_views(low) + sum_views(low), plain_views(hi[i]) + sum_views(hi[i]))
                    for k, ((dst, src), (high, _)) in enumerate(views):
                        dve.wait_ge(s_h, n * 6 + k + 1 + START)
                        v.tensor_tensor(dst, src, high, ALU.subtract).then_inc(s_l, 1)

                def partial(m):
                    n = b * SS + m
                    quarter = ob.rearrange("p (k s j c) -> p s c k j", s=2, j=HC, c=2)
                    bank = lambda q: ps[0:C, PSBANK[TIME[q]], 0:OUTS]
                    dve.wait_ge(s_m0, n + 1 + START)
                    for c in range(2):
                        dve.wait_ge(s_cv, n * 9 + 2 + c + START)
                        v.scalar_tensor_tensor(mid[1 + c], bank(1 + c), col(OSC), mid[0], ALU.mult, ALU.add).then_inc(s_mid, 1)
                    dve.wait_ge(s_mid, n * SV + 2 + START)
                    dve.wait_ge(s_out, n * 16 + START)
                    for s_ in range(2):
                        dve.wait_ge(s_cv, n * 9 + 4 + s_ + START)
                        for c in range(2):
                            v.scalar_tensor_tensor(quarter[:, s_, c], bank(3 + s_).rearrange("p (k j) -> p k j", j=HC), col(OSC),
                                                   mid[1 + c].rearrange("p (k j) -> p k j", j=HC),
                                                   ALU.mult, ALU.add).then_inc(s_mid, 1)

                def final(m):
                    n = b * SS + m
                    quarter = ob.rearrange("p (k s j c) -> p s c k j", s=2, j=HC, c=2)
                    dve.wait_ge(s_res, n + 1 + START)
                    for s_ in range(2):
                        for c in range(2):
                            q = 5 + 2 * s_ + c
                            dve.wait_ge(s_cv, n * 9 + q + 1 + START)
                            v.scalar_tensor_tensor(quarter[:, s_, c], ps[0:C, PSBANK[TIME[q]], 0:OUTS].rearrange("p (k j) -> p k j", j=HC),
                                                   col(OSC), quarter[:, s_, c], ALU.mult, ALU.add).then_inc(s_mid, 1)

                def next_statistics(m, i, count):
                    with dve.If(b < B - 1):
                        dve.wait_ge(s_x[i], (b * (SS // 2) + count) * 16 + START)
                        statistics(m)

                def unit_pair(m2, first):
                    for i in range(2):
                        m = m2 * 2 + i
                        partial(m)
                        sums(m + 2)
                        if not (first and i == 0):
                            next_statistics(m - 1, 1 - i, m2 + i)
                        final(m)
                        lows(m + 2, i, m2 + 1 + i)
                sums(0)
                lows(0, 0, 0)
                sums(1)
                lows(1, 1, 1)
                unit_pair(0, True)
                with dve.Fori(1, SS // 2 - 1) as m2:
                    unit_pair(m2, False)
                for i in range(2):
                    m = SS - 2 + i
                    partial(m)
                    next_statistics(m - 1, 1 - i, SS // 2 - 1 + i)
                    final(m)
                next_statistics(SS - 1, 1, SS // 2)


_INS = ['x', 'L0_conv_ln_w', 'L0_conv_ln_b', 'L0_conv_q_w', 'L0_conv_q_dw', 'L0_conv_kv_w', 'L0_conv_kv_dw',
        'L0_conv_proj_w', 'L0_conv_temperature', 'L1_conv_w1', 'L1_conv_w3', 'L1_conv_w5', 'L1_conv_wd', 'L1_conv_wf']


def kernel(**inputs):
    import numpy as _np
    import concourse.bacc as _bacc
    from concourse import mybir as _mybir
    from concourse.bass_utils import run_bass_kernel_spmd as _run

    nc = _bacc.Bacc("TRN2", target_bir_lowering=False, num_devices=1)
    arrays, args = {}, []
    for name in _INS:
        a = _np.ascontiguousarray(inputs[name])
        arrays[f"in_{name}_dram"] = a
        args.append(nc.dram_tensor(f"in_{name}_dram", a.shape, _mybir.dt.from_np(a.dtype), kind="ExternalInput").ap())
    shape = inputs['x'].shape
    args.append(nc.dram_tensor("out_0_dram", shape, _mybir.dt.float32, kind="ExternalOutput").ap())
    build_program(nc, *args)
    r = _run(nc, [arrays], core_ids=[0])
    return r.results[0]["out_0_dram"]
```
